# Optimizing a Trainium2 kernel written in Bass

```python
import numpy as np
import jax
import jax.numpy as jnp

def _softmax(x, axis=-1):
    return jax.nn.softmax(x, axis=axis)

def _gelu(x):
    return jax.nn.gelu(x, approximate=True)

def _silu(x):
    return jax.nn.silu(x)

def _sigmoid(x):
    return jax.nn.sigmoid(x)

def _layernorm(x, axis=-1, eps=1e-05):
    m = jnp.mean(x, axis=axis, keepdims=True)
    v = jnp.var(x, axis=axis, keepdims=True)
    return (x - m) / jnp.sqrt(v + eps)

def _scatter_add(tgt, idx, src, axis=0):
    return tgt.at[idx].add(src)

def _segment_sum(src, seg, n):
    return jax.ops.segment_sum(src, seg, n)
kernel_name = 'mk_gnn_preln_d4_gnn_r32_15b188'

def setup_inputs(seed: int=0):
    np.random.seed(seed)
    _w = jnp.asarray

    def _rec_inputs():
        import jax
        import jax.numpy as jnp
        _gk = jax.random.key(seed)
        x = -0.0003713 + 1 * jax.random.normal(jax.random.fold_in(_gk, 1), (3125, 128), jnp.float32)
        src = jax.random.randint(jax.random.fold_in(_gk, 2), (100000,), 0, 3125, jnp.int32)
        dst = jnp.minimum((3125 * jax.random.uniform(jax.random.fold_in(_gk, 3), (100000,)) ** 2.0).astype(jnp.int32), 99999)
        _o = jnp.argsort(dst, stable=True)
        src = src[_o]
        dst = dst[_o]
        edge_attr_32 = 0.000196303 + 1.00016 * jax.random.normal(jax.random.fold_in(_gk, 12), (100000, 32), jnp.float32)
        edge_type_16 = jax.random.randint(jax.random.fold_in(_gk, 14), (100000,), 0, 16, jnp.int32)
        return (x, src, dst, edge_attr_32, edge_type_16)
    x, src, dst, edge_attr_32, edge_type_16 = _rec_inputs()

    def _L0_gnn_setup():
        import jax, jax.numpy as jnp
        import numpy as np
        N_NODES = 3125
        N_EDGES = 18750
        D_IN = 128
        D_OUT = 128
        N_REL = 16
        N_BASES = 2
        key = jax.random.key(seed)
        k1, k2, k3, k4, k5, k6 = jax.random.split(key, 6)
        x = jax.random.normal(k1, (N_NODES, D_IN), dtype=jnp.float32)
        edge_idx = jax.random.randint(k2, (2, N_EDGES), 0, N_NODES, dtype=jnp.int32)
        edge_type = jax.random.randint(k3, (N_EDGES,), 0, N_REL, dtype=jnp.int32)
        self_weight = jax.random.normal(k4, (D_IN, D_OUT), dtype=jnp.float32) * (2.0 / D_IN) ** 0.5
        bases = jax.random.normal(k5, (N_BASES, D_IN, D_OUT), dtype=jnp.float32) * (2.0 / (D_IN + D_OUT)) ** 0.5
        base_weights = jax.random.normal(k6, (N_REL, N_BASES), dtype=jnp.float32) * (2.0 / (N_REL + N_BASES)) ** 0.5
        return {'x': x, 'edge_idx': edge_idx, 'edge_type': edge_type, 'self_weight': self_weight, 'bases': bases, 'base_weights': base_weights}
    _L0_gnn_all = _L0_gnn_setup()
    _L0_gnn_in = {k: v for k, v in _L0_gnn_all.items() if k in ('self_weight', 'bases', 'base_weights')}
    del _L0_gnn_all

    def _L1_gnn_setup():
        import jax, jax.numpy as jnp
        import numpy as np
        N = 3125
        E = 18750
        D_IN = 128
        D = 128
        L = 3

        def gru_cell(m, h, w_ih, w_hh, b_ih, b_hh):
            gi = m @ w_ih.T + b_ih
            gh = h @ w_hh.T + b_hh
            ir, iz, inn = jnp.split(gi, 3, axis=-1)
            hr, hz, hn = jnp.split(gh, 3, axis=-1)
            r = jax.nn.sigmoid(ir + hr)
            z = jax.nn.sigmoid(iz + hz)
            n = jnp.tanh(inn + r * hn)
            return (1.0 - z) * n + z * h
        key = jax.random.key(seed)
        ks = jax.random.split(key, 10)
        s = 1.0 / np.sqrt(D)
        x = jax.random.normal(ks[0], (N, D_IN), dtype=jnp.float32)
        edge_index = jax.random.randint(ks[1], (2, E), 0, N, dtype=jnp.int64)
        lin_w = jax.random.normal(ks[2], (D, D_IN), dtype=jnp.float32) * (1.0 / np.sqrt(D_IN))
        lin_b = jnp.zeros((D,), dtype=jnp.float32)
        weight = jax.random.normal(ks[3], (L, D, D), dtype=jnp.float32) * s
        w_ih = jax.random.normal(ks[4], (3 * D, D), dtype=jnp.float32) * s
        w_hh = jax.random.normal(ks[5], (3 * D, D), dtype=jnp.float32) * s
        b_ih = jnp.zeros((3 * D,), dtype=jnp.float32)
        b_hh = jnp.zeros((3 * D,), dtype=jnp.float32)
        return {'x': x, 'lin_w': lin_w, 'lin_b': lin_b, 'weight': weight, 'w_ih': w_ih, 'w_hh': w_hh, 'b_ih': b_ih, 'b_hh': b_hh, 'edge_index': edge_index}
    _L1_gnn_all = _L1_gnn_setup()
    _L1_gnn_in = {k: v for k, v in _L1_gnn_all.items() if k in ('lin_w', 'lin_b', 'weight', 'w_ih', 'w_hh', 'b_ih', 'b_hh')}
    del _L1_gnn_all

    def _L2_gnn_setup():
        import jax, jax.numpy as jnp
        import numpy as np
        EPS = 1e-12
        key = jax.random.key(seed)
        k1, k2, k3, k4, k5 = jax.random.split(key, 5)
        N, E, D_IN, D_OUT = (3125, 50000, 128, 128)
        features = jax.random.normal(k1, (N, D_IN), dtype=jnp.float32)
        W = jax.random.normal(k2, (D_OUT, D_IN), dtype=jnp.float32) * 0.05
        b = jax.random.normal(k3, (D_OUT,), dtype=jnp.float32) * 0.05
        src = jax.random.randint(k4, (E,), 0, N, dtype=jnp.int32)
        dst = jax.random.randint(k5, (E,), 0, N, dtype=jnp.int32)
        return {'features': features, 'W': W, 'b': b, 'src': src, 'dst': dst}
    _L2_gnn_all = _L2_gnn_setup()
    _L2_gnn_in = {k: v for k, v in _L2_gnn_all.items() if k in ('W', 'b')}
    del _L2_gnn_all

    def _L3_gnn_setup():
        import jax, jax.numpy as jnp
        import numpy as np
        N_NODES = 50000
        N_EDGES = 25000
        IN_F = 128
        OUT_F = 128
        HEADS = 8
        HEAD_DIM = OUT_F // HEADS
        EDGE_F = 32
        key = jax.random.key(seed)
        ks = jax.random.split(key, 14)
        s = lambda fan_in: 1.0 / np.sqrt(fan_in)
        return {'node_features': jax.random.normal(ks[0], (N_NODES, IN_F), jnp.float32), 'edge_index': jax.random.randint(ks[1], (2, N_EDGES), 0, N_NODES, jnp.int64), 'edge_features': jax.random.normal(ks[2], (N_EDGES, EDGE_F), jnp.float32), 'Wq': jax.random.uniform(ks[3], (IN_F, OUT_F), jnp.float32, -s(IN_F), s(IN_F)), 'bq': jnp.zeros((OUT_F,), jnp.float32), 'Wk': jax.random.uniform(ks[4], (IN_F, OUT_F), jnp.float32, -s(IN_F), s(IN_F)), 'bk': jnp.zeros((OUT_F,), jnp.float32), 'Wv': jax.random.uniform(ks[5], (IN_F, OUT_F), jnp.float32, -s(IN_F), s(IN_F)), 'bv': jnp.zeros((OUT_F,), jnp.float32), 'We': jax.random.uniform(ks[6], (EDGE_F, HEADS), jnp.float32, -s(EDGE_F), s(EDGE_F)), 'be': jnp.zeros((HEADS,), jnp.float32), 'Wo': jax.random.uniform(ks[7], (OUT_F, OUT_F), jnp.float32, -s(OUT_F), s(OUT_F)), 'bo': jnp.zeros((OUT_F,), jnp.float32)}
    _L3_gnn_all = _L3_gnn_setup()
    _L3_gnn_in = {k: v for k, v in _L3_gnn_all.items() if k in ('Wq', 'bq', 'Wk', 'bk', 'Wv', 'bv', 'We', 'be', 'Wo', 'bo')}
    del _L3_gnn_all
    return {'x': x, 'src': src, 'dst': dst, 'edge_attr_32': edge_attr_32, 'edge_type_16': edge_type_16, 'L0_gnn_self_weight': _L0_gnn_in['self_weight'], 'L0_gnn_bases': _L0_gnn_in['bases'], 'L0_gnn_base_weights': _L0_gnn_in['base_weights'], 'L1_gnn_lin_w': _L1_gnn_in['lin_w'], 'L1_gnn_lin_b': _L1_gnn_in['lin_b'], 'L1_gnn_weight': _L1_gnn_in['weight'], 'L1_gnn_w_ih': _L1_gnn_in['w_ih'], 'L1_gnn_w_hh': _L1_gnn_in['w_hh'], 'L1_gnn_b_ih': _L1_gnn_in['b_ih'], 'L1_gnn_b_hh': _L1_gnn_in['b_hh'], 'L2_gnn_W': _L2_gnn_in['W'], 'L2_gnn_b': _L2_gnn_in['b'], 'L3_gnn_Wq': _L3_gnn_in['Wq'], 'L3_gnn_bq': _L3_gnn_in['bq'], 'L3_gnn_Wk': _L3_gnn_in['Wk'], 'L3_gnn_bk': _L3_gnn_in['bk'], 'L3_gnn_Wv': _L3_gnn_in['Wv'], 'L3_gnn_bv': _L3_gnn_in['bv'], 'L3_gnn_We': _L3_gnn_in['We'], 'L3_gnn_be': _L3_gnn_in['be'], 'L3_gnn_Wo': _L3_gnn_in['Wo'], 'L3_gnn_bo': _L3_gnn_in['bo']}

def reference(x, src, dst, edge_attr_32, edge_type_16, L0_gnn_self_weight, L0_gnn_bases, L0_gnn_base_weights, L1_gnn_lin_w, L1_gnn_lin_b, L1_gnn_weight, L1_gnn_w_ih, L1_gnn_w_hh, L1_gnn_b_ih, L1_gnn_b_hh, L2_gnn_W, L2_gnn_b, L3_gnn_Wq, L3_gnn_bq, L3_gnn_Wk, L3_gnn_bk, L3_gnn_Wv, L3_gnn_bv, L3_gnn_We, L3_gnn_be, L3_gnn_Wo, L3_gnn_bo):
    import jax
    import jax.numpy as jnp

    def _L0_gnn_ref(x, edge_idx, edge_type, self_weight, bases, base_weights):
        import jax, jax.numpy as jnp
        import numpy as np
        N_NODES = 3125
        N_EDGES = 18750
        D_IN = 128
        D_OUT = 128
        N_REL = 16
        N_BASES = 2
        heads = edge_idx[0]
        tails = edge_idx[1]
        gathered = x[heads]
        n_rel = base_weights.shape[0]

        def work_relation(acc, rel_inputs):
            rel, coef = rel_inputs
            rel_mask = (edge_type == rel)[:, None]
            msgs = jnp.where(rel_mask, gathered, 0.0)
            scattered = jnp.zeros_like(x).at[tails].add(msgs)
            w_rel = jnp.einsum('b,bio->io', coef, bases)
            return (acc + scattered @ w_rel, None)
        init = jnp.zeros((x.shape[0], bases.shape[2]), dtype=x.dtype)
        rel_out, _ = jax.lax.scan(work_relation, init, (jnp.arange(n_rel, dtype=edge_type.dtype), base_weights))
        return x @ self_weight + rel_out

    def _L1_gnn_ref(x, lin_w, lin_b, weight, w_ih, w_hh, b_ih, b_hh, edge_index):
        import jax, jax.numpy as jnp
        import numpy as np
        N = 3125
        E = 18750
        D_IN = 128
        D = 128
        L = 3

        def gru_cell(m, h, w_ih, w_hh, b_ih, b_hh):
            gi = m @ w_ih.T + b_ih
            gh = h @ w_hh.T + b_hh
            ir, iz, inn = jnp.split(gi, 3, axis=-1)
            hr, hz, hn = jnp.split(gh, 3, axis=-1)
            r = jax.nn.sigmoid(ir + hr)
            z = jax.nn.sigmoid(iz + hz)
            n = jnp.tanh(inn + r * hn)
            return (1.0 - z) * n + z * h
        h = x @ lin_w.T + lin_b
        src, dst = (edge_index[0], edge_index[1])
        n_nodes = h.shape[0]
        for i in range(weight.shape[0]):
            m = h @ weight[i]
            agg = jax.ops.segment_sum(m[src], dst, num_segments=n_nodes)
            h = gru_cell(agg, h, w_ih, w_hh, b_ih, b_hh)
        return h

    def _L2_gnn_ref(features, W, b, src, dst):
        import jax, jax.numpy as jnp
        import numpy as np
        EPS = 1e-12
        N = features.shape[0]
        neigh_sum = jax.ops.segment_sum(features[src], dst, num_segments=N)
        total = jnp.sum(features, axis=0)
        h_NN = total[None, :] - neigh_sum
        norm = jnp.sqrt(jnp.sum(h_NN * h_NN, axis=1, keepdims=True))
        h_norm = h_NN / jnp.maximum(norm, EPS)
        return h_norm @ W.T + b

    def _L3_gnn_ref(node_features, edge_index, edge_features, Wq, bq, Wk, bk, Wv, bv, We, be, Wo, bo):
        import jax, jax.numpy as jnp
        import numpy as np
        N_NODES = 50000
        N_EDGES = 25000
        IN_F = 128
        OUT_F = 128
        HEADS = 8
        HEAD_DIM = OUT_F // HEADS
        EDGE_F = 32
        n_nodes = node_features.shape[0]
        n_edges = edge_index.shape[1]
        sources, targets = (edge_index[0], edge_index[1])
        scale = HEAD_DIM ** (-0.5)
        Q = (node_features @ Wq + bq).reshape(n_nodes, HEADS, HEAD_DIM)
        K = (node_features @ Wk + bk).reshape(n_nodes, HEADS, HEAD_DIM)
        V = (node_features @ Wv + bv).reshape(n_nodes, HEADS, HEAD_DIM)
        Q_t = Q[targets]
        K_s = K[sources]
        V_s = V[sources]
        scores = jnp.sum(Q_t * K_s, axis=-1) * scale
        scores = scores + (edge_features @ We + be)
        max_s = jax.ops.segment_max(scores, targets, num_segments=n_nodes)
        scores = scores - max_s[targets]
        exp_s = jnp.exp(scores)
        denom = jax.ops.segment_sum(exp_s, targets, num_segments=n_nodes) + 1e-10
        probs = exp_s / denom[targets]
        weighted_V = probs[:, :, None] * V_s
        aggregated = jax.ops.segment_sum(weighted_V.reshape(n_edges, -1), targets, num_segments=n_nodes)
        return aggregated @ Wo + bo
    edge_index = jnp.stack([src, dst])
    h = jnp.maximum(_layernorm(x, axis=-1), 0.0)
    x = x + _L0_gnn_ref(h, edge_index, edge_type_16, L0_gnn_self_weight, L0_gnn_bases, L0_gnn_base_weights)
    h = jnp.maximum(_layernorm(x, axis=-1), 0.0)
    x = x + _L1_gnn_ref(h, L1_gnn_lin_w, L1_gnn_lin_b, L1_gnn_weight, L1_gnn_w_ih, L1_gnn_w_hh, L1_gnn_b_ih, L1_gnn_b_hh, edge_index)
    h = jnp.maximum(_layernorm(x, axis=-1), 0.0)
    x = x + _L2_gnn_ref(h, L2_gnn_W, L2_gnn_b, src, dst)
    h = jnp.maximum(_layernorm(x, axis=-1), 0.0)
    x = x + _L3_gnn_ref(h, edge_index, edge_attr_32, L3_gnn_Wq, L3_gnn_bq, L3_gnn_Wk, L3_gnn_bk, L3_gnn_Wv, L3_gnn_bv, L3_gnn_We, L3_gnn_be, L3_gnn_Wo, L3_gnn_bo)
    return x

_drawn_inputs = setup_inputs


def setup_inputs(seed=0):
    import zlib

    import numpy as np

    out = dict(_drawn_inputs(seed))
    spreads = {'L1_gnn_lin_b': (0.0, 0.1),
     'L1_gnn_b_ih': (0.0, 0.274),
     'L1_gnn_b_hh': (0.0, 0.27),
     'L3_gnn_bq': (0.0, 2.0),
     'L3_gnn_bk': (0.0, 2.0),
     'L3_gnn_bv': (0.0, 0.642),
     'L3_gnn_be': (0.0, 2.0),
     'L3_gnn_bo': (0.0, 0.332)}
    factors = {'edge_attr_32': 8.0,
     'L2_gnn_W': 4.539,
     'L2_gnn_b': 4.67,
     'L3_gnn_Wq': 24.756,
     'L3_gnn_Wk': 23.93,
     'L3_gnn_We': 8.0}
    for name, (base, spread) in spreads.items():
        noise = np.random.default_rng([zlib.crc32(name.encode()), seed]).standard_normal(out[name].shape)
        drawn = base * np.exp(spread * noise) if base else spread * noise
        out[name] = jnp.asarray(drawn.astype(out[name].dtype))
    for name, factor in factors.items():
        out[name] = (out[name] * factor).astype(out[name].dtype)
    return out
```

```python
import concourse.bass as bass
from concourse import mybir
from contextlib import ExitStack

F32, F16, BF16, I32 = mybir.dt.float32, mybir.dt.float16, mybir.dt.bfloat16, mybir.dt.int32
ALU = mybir.AluOpType
ACT = mybir.ActivationFunctionType
AX = mybir.AxisListType

P = 128
D = 128
N_NODES = 3125
N_EDGES = 100000
BLOCKS = -(-N_NODES // P)
NODES = BLOCKS * P
LAST_ROWS = N_NODES - (BLOCKS - 1) * P
GROUP = 16
TILES = -(-N_EDGES // (P * GROUP)) * GROUP
GROUPS = TILES // GROUP
PAIRS = TILES // 2
PAIRS_IN_GROUP = GROUP // 2
EDGES = TILES * P
PAIR_EDGES = 2 * P
SRC_W = 3136
CENTER = 1600
NO_NODE = 4095
RELATIONS, BASES = 16, 2
HEADS, HEAD_DIM, EDGE_F = 8, 16, 32
LN_EPS = 1e-5
BANK = 512
CHUNKS = [(c * 4, min(4, BLOCKS - c * 4)) for c in range(-(-BLOCKS // 4))]


class Count:

    def __init__(self, sem):
        self.sem, self.n = sem, 0

    def up(self, by=1):
        self.n += by
        return self.n


class Stage:

    used = []

    def __init__(self, nc, name):
        self.nc, self.name, self.ctx = nc, name, ExitStack()

    def __enter__(self):
        self.ctx.__enter__()
        return self

    def __exit__(self, *exc):
        return self.ctx.__exit__(*exc)

    def sb(self, name, shape, dt=F32):
        return self.ctx.enter_context(self.nc.sbuf_tensor(f"{self.name}_sb_{name}", shape, dt))

    def ps(self, name, shape, dt=F32):
        return self.ctx.enter_context(self.nc.psum_tensor(f"{self.name}_ps_{name}", shape, dt))

    def sem(self, name):
        Stage.used.append(self.nc.alloc_semaphore(f"{self.name}_{name}"))
        return Stage.used[-1]

    @staticmethod
    def clear_semaphores(nc):
        nc.clear_and_free_semaphores(Stage.used)
        nc.all_engine_barrier()
        Stage.used = []


def rows(table):
    return table.rearrange("(k p) f -> p k f", p=P)



class NormBuffers:
    def __init__(self, st):
        self.stats = st.sb("ln_stats", [P, BLOCKS, 6])
        self.total = st.sb("ln_total", [P, BLOCKS])
        self.diff = st.sb("ln_diff", [P, BLOCKS])
        self.square = st.sb("ln_square", [P, BLOCKS])
        self.m2 = st.sb("ln_m2", [P, BLOCKS])
        self.var = st.sb("ln_var", [P, BLOCKS])
        self.std = st.sb("ln_std", [P, BLOCKS])
        self.rstd = st.sb("ln_rstd", [P, BLOCKS])
        self.shift = st.sb("ln_shift", [P, BLOCKS])
        self.eps = st.sb("ln_eps", [P, 1])
        self.step = Count(st.sem("ln_step"))
        self.var_ready = st.sem("ln_var_ready")
        self.std_ready = st.sem("ln_std_ready")
        self.scale_ready = st.sem("ln_scale_ready")


def norm_vector(vector, ln, x):
    step = ln.step
    vector.memset(ln.eps[:, :], LN_EPS)
    with vector.Fori(0, BLOCKS) as b:
        vector.bn_stats(ln.stats[:, bass.ds(b, 1), :], x[:, bass.ds(b, 1), :]).then_inc(step.sem, 1)
    vector.wait_ge(step.sem, step.up(BLOCKS))
    mean_e, mean_o = ln.stats[:, :, 1], ln.stats[:, :, 4]
    vector.tensor_tensor(ln.total[:, :], mean_e, mean_o, ALU.add).then_inc(step.sem, 1)
    vector.tensor_tensor(ln.diff[:, :], mean_e, mean_o, ALU.subtract).then_inc(step.sem, 1)
    vector.tensor_tensor(ln.m2[:, :], ln.stats[:, :, 2], ln.stats[:, :, 5], ALU.add).then_inc(step.sem, 1)
    vector.wait_ge(step.sem, step.up(3))
    vector.tensor_tensor(ln.square[:, :], ln.diff[:, :], ln.diff[:, :], ALU.mult).then_inc(step.sem, 1)
    vector.wait_ge(step.sem, step.up())
    vector.scalar_tensor_tensor(ln.var[:, :], ln.square[:, :], D / 4.0, ln.m2[:, :],
                                ALU.mult, ALU.add).then_inc(ln.var_ready, 1)
    vector.wait_ge(ln.std_ready, 1)
    vector.reciprocal(ln.rstd[:, :], ln.std[:, :]).then_inc(step.sem, 1)
    vector.wait_ge(step.sem, step.up())
    vector.scalar_tensor_tensor(ln.shift[:, :], ln.total[:, :], -0.5, ln.rstd[:, :],
                                ALU.mult, ALU.mult).then_inc(ln.scale_ready, 1)


def norm_scalar(scalar, ln, x, h, h_ready):
    scalar.wait_ge(ln.var_ready, 1)
    scalar.activation(ln.std[:, :], ln.var[:, :], ACT.Sqrt, bias=ln.eps[:, 0:1],
                      scale=1.0 / D).then_inc(ln.std_ready, 1)
    scalar.wait_ge(ln.scale_ready, 1)
    with scalar.Fori(0, BLOCKS) as b:
        scalar.activation(h[:, bass.ds(b, 1), :], x[:, bass.ds(b, 1), :], ACT.Relu,
                          bias=ln.shift[:, bass.ds(b, 1)], scale=ln.rstd[:, bass.ds(b, 1)]).then_inc(h_ready, 1)



class Edges:

    def __init__(self, nc, ctx):
        def sb(name, shape, dt):
            return ctx.enter_context(nc.sbuf_tensor(name, shape, dt))

        self.nc = nc
        self.first_pair = sb("first_pair", [1, BLOCKS + 1], I32)
        self.ident = sb("ident", [P, P], F32)
        self.ident16 = sb("ident16", [P, P], BF16)

    def columns(self, ctx, name):
        self.src, self.dst = (ctx.enter_context(self.nc.sbuf_tensor(f"{name}_edge_{n}", [P, TILES], F16))
                              for n in ("src", "dst"))


def prepare(nc, edges, io, dr):
    with Stage(nc, "prep") as st:
        edges.columns(st.ctx, "prep")
        src_i = st.sb("src_i", [P, TILES], I32)
        dst_i = st.sb("dst_i", [P, TILES], I32)
        type_i = st.sb("type_i", [P, TILES], I32)
        dst_f = st.sb("dst_f", [P, TILES])
        type_h = st.sb("type_h", [P, TILES], F16)
        junk = st.sb("junk", [P, 2, TILES], F16)
        is_rel = st.sb("is_rel", [P, 2, TILES], F16)
        below = st.sb("below", [P, BLOCKS - 1])
        pair = st.sb("pair", [1, BLOCKS - 1])
        pair_c = st.sb("pair_c", [1, BLOCKS - 1])
        first_f = st.sb("first_f", [1, BLOCKS + 1])
        ones = st.sb("ones", [P, P])
        rel_w = st.sb("rel_w", [P, RELATIONS * BASES])
        coef = st.sb("coef", [P, BASES, TILES])
        x = st.sb("x", [P, BLOCKS, D])
        h = st.sb("h", [P, BLOCKS, D])
        h_t = st.sb("h_t", [P, NODES])
        self_w = st.sb("self_w", [D, D])
        attr = [st.sb(f"attr{i}", [P, 16, P]) for i in range(2)]
        we = st.sb("we", [EDGE_F * 4, 4 * HEADS])
        be = st.sb("be", [P, HEADS])
        bias = st.sb("bias", [P, GROUPS, HEADS, GROUP])
        ln = NormBuffers(st)
        p_below = st.ps("p_below", [P, BANK])
        p_turn = [st.ps(f"p_turn{i}", [P, BANK]) for i in range(2)]
        p_self = [st.ps(f"p_self{i}", [P, BANK]) for i in range(2)]
        p_bias = [st.ps(f"p_bias{i}", [P, BANK]) for i in range(2)]

        edges_in, x_in, w_in, relw_in = (st.sem(n) for n in ("edges_in", "x_in", "w_in", "relw_in"))
        attr_in = [st.sem(f"attr_in{i}") for i in range(2)]
        const_ready = st.sem("const_ready")
        ident_step = st.sem("ident_step")
        we_clear = st.sem("we_clear")
        v_step = Count(st.sem("v_step"))
        below_ready, below_summed = st.sem("below_ready"), st.sem("below_summed")
        h_ready = st.sem("h_ready")
        turned, turned_out = st.sem("turned"), st.sem("turned_out")
        selfed, selfed_out = st.sem("selfed"), st.sem("selfed_out")
        bias_made, bias_out = st.sem("bias_made"), st.sem("bias_out")
        stored = st.sem("stored")
        coef_ready = st.sem("coef_ready")
        columns_ready = st.sem("columns_ready")

        QUADS = TILES // 4
        LOTS = [(q, min(16, QUADS - q)) for q in range(0, QUADS, 16)]

        with nc.Block() as block:
            @block.sync
            def _(sync):
                sync.dma_start(dst_i[:, :], io["dst"]).then_inc(edges_in, 16)
                sync.dma_start(src_i[:, :], io["src"]).then_inc(edges_in, 16)
                sync.dma_start(type_i[:, :], io["etype"]).then_inc(edges_in, 16)
                sync.dma_start(x[:, :, :], rows(io["x"])).then_inc(x_in, 16)
                sync.dma_start(self_w[:, :], io["self_w"]).then_inc(w_in, 16)
                sync.dma_start(rel_w[:, :], io["rel_w"].partition_broadcast(P)).then_inc(relw_in, 16)
                sync.dma_start(be[:, :], io["be"].partition_broadcast(P)).then_inc(relw_in, 16)
                sync.wait_ge(we_clear, 1)
                for j in range(4):
                    sync.dma_start(we[j * EDGE_F:(j + 1) * EDGE_F, j * HEADS:(j + 1) * HEADS],
                                   io["we"]).then_inc(w_in, 16)
                for i, (q, n) in enumerate(LOTS):
                    if i >= 2:
                        sync.wait_ge(bias_made, i - 1)
                    sync.dma_start(attr[i % 2][:, 0:n, :], io["attr"][:, q:q + n, :]).then_inc(attr_in[i % 2], 16)
                sync.wait_ge(columns_ready, 2)
                sync.dma_start(dr["src"], edges.src[:, :]).then_inc(stored, 16)
                sync.dma_start(dr["dst"], edges.dst[:, :]).then_inc(stored, 16)
                sync.wait_ge(h_ready, BLOCKS)
                sync.dma_start(rows(dr["h0"]), h[:, :, :]).then_inc(stored, 16)
                sync.wait_ge(selfed_out, len(CHUNKS))
                sync.dma_start(rows(dr["x0"]), x[:, :, :]).then_inc(stored, 16)
                sync.wait_ge(coef_ready, BASES)
                sync.dma_start(dr["coef"], coef[:, :, :]).then_inc(stored, 16)
                sync.wait_ge(bias_out, len(LOTS))
                sync.dma_start(dr["bias"], bias[:, :, :, :].rearrange("p g h t -> p (g h t)")).then_inc(stored, 16)
                sync.wait_ge(stored, 96)

            @block.gpsimd
            def _(gpsimd):
                gpsimd.memset(we[:, :], 0.0).then_inc(we_clear, 1)
                gpsimd.memset(ones[:, :], 1.0).then_inc(const_ready, 1)
                for n, ident in enumerate((edges.ident, edges.ident16)):
                    gpsimd.memset(ident[:, :], 0.0).then_inc(ident_step, 1)
                    gpsimd.wait_ge(ident_step, n + 1)
                    gpsimd.affine_select(out=ident[:, :], in_=ident[:, :], compare_op=ALU.not_equal, fill=1.0,
                                         base=0, pattern=[[-1, P]], channel_multiplier=1).then_inc(const_ready, 1)

            @block.vector
            def _(vector):
                vector.wait_ge(edges_in, 48)
                vector.tensor_copy(dst_f[:, :], dst_i[:, :]).then_inc(v_step.sem, 1)
                vector.tensor_scalar(edges.dst[:, :], dst_i[:, :], -CENTER, None, ALU.add).then_inc(columns_ready, 1)
                vector.tensor_scalar(edges.src[:, :], src_i[:, :], -CENTER, None, ALU.add).then_inc(columns_ready, 1)
                vector.tensor_copy(type_h[:, :], type_i[:, :]).then_inc(v_step.sem, 1)
                vector.wait_ge(v_step.sem, v_step.up(2))
                for b in range(BLOCKS - 1):
                    if b >= 2:
                        vector.wait_ge(v_step.sem, v_step.n - 1)
                    vector.tensor_scalar(junk[:, b % 2, :], dst_f[:, :], float(P * (b + 1)), 0.0, ALU.is_lt,
                                         ALU.add, accum_out=below[:, b:b + 1]).then_inc(v_step.sem, 1)
                    v_step.up()
                vector.wait_ge(v_step.sem, v_step.n)
                vector.memset(first_f[:, :], 0.0).then_inc(below_ready, 1)
                vector.wait_ge(x_in, 16)
                norm_vector(vector, ln, x)
                vector.wait_ge(below_summed, 1)
                vector.tensor_scalar(pair[:, :], p_below[0:1, 0:BLOCKS - 1], 1.0 / PAIR_EDGES,
                                     -1.0 / PAIR_EDGES - (PAIR_EDGES / 2 - 0.5) / PAIR_EDGES,
                                     ALU.mult, ALU.add).then_inc(v_step.sem, 1)
                vector.wait_ge(v_step.sem, v_step.up())
                vector.tensor_scalar(pair_c[:, :], pair[:, :], 0.0, 2.0 ** 23, ALU.max, ALU.add)\
                      .then_inc(v_step.sem, 1)
                vector.wait_ge(v_step.sem, v_step.up())
                vector.tensor_scalar(first_f[:, 1:BLOCKS], pair_c[:, :], -2.0 ** 23, None, ALU.add)\
                      .then_inc(v_step.sem, 1)
                vector.memset(first_f[:, BLOCKS:BLOCKS + 1], float(PAIRS - 1)).then_inc(v_step.sem, 1)
                vector.wait_ge(v_step.sem, v_step.up(2))
                vector.tensor_copy(edges.first_pair[:, :], first_f[:, :]).then_inc(v_step.sem, 1)
                v_step.up()
                for c, (b, n) in enumerate(CHUNKS):
                    vector.wait_ge(selfed, c + 1)
                    vector.tensor_tensor(x[:, b:b + n, :], x[:, b:b + n, :],
                                         p_self[c % 2][:, 0:n * D].rearrange("p (k f) -> p k f", f=D),
                                         ALU.add).then_inc(selfed_out, 1)
                vector.wait_ge(relw_in, 32)
                for r in range(RELATIONS):
                    if r >= 2:
                        vector.wait_ge(v_step.sem, v_step.n)
                    vector.tensor_scalar(is_rel[:, r % 2, :], type_h[:, :], float(r), None, ALU.is_equal)\
                          .then_inc(v_step.sem, 1)
                    vector.wait_ge(v_step.sem, v_step.up())
                    for a in range(BASES):
                        w = rel_w[:, BASES * r + a:BASES * r + a + 1]
                        if r == 0:
                            vector.tensor_scalar(coef[:, a, :], is_rel[:, 0, :], w, None, ALU.mult)\
                                  .then_inc(v_step.sem, 1)
                        else:
                            vector.scalar_tensor_tensor(coef[:, a, :], is_rel[:, r % 2, :], w, coef[:, a, :],
                                                        ALU.mult, ALU.add)\
                                  .then_inc(coef_ready if r == RELATIONS - 1 else v_step.sem, 1)
                        v_step.up()
                for i, (q, n) in enumerate(LOTS):
                    g, m = q // 4, n // 4
                    vector.wait_ge(bias_made, i + 1)
                    vector.tensor_tensor(bias[:, g:g + m, :, :].rearrange("p g h t -> p g t h"),
                                         p_bias[i % 2][:, 0:n * 32].rearrange("p (g t h) -> p g t h", t=GROUP, h=HEADS),
                                         be[:, :].unsqueeze(1).unsqueeze(1).broadcast_to([P, m, GROUP, HEADS]),
                                         ALU.add).then_inc(bias_out, 1)

            @block.scalar
            def _(scalar):
                norm_scalar(scalar, ln, x, h, h_ready)
                for c, (b, n) in enumerate(CHUNKS):
                    scalar.wait_ge(turned, c + 1)
                    scalar.activation(h_t[:, b * P:(b + n) * P], p_turn[c % 2][:, 0:n * P], ACT.Copy)\
                          .then_inc(turned_out, 1)

            @block.tensor
            def _(tensor):
                tensor.wait_ge(const_ready, 3)
                tensor.wait_ge(below_ready, 1)
                tensor.matmul(p_below[:, 0:BLOCKS - 1], ones[:, :], below[:, :], start=True, stop=True)\
                      .then_inc(below_summed, 1)
                tensor.wait_ge(w_in, 5 * 16)

                def self_product(c):
                    b, n = CHUNKS[c]
                    tensor.wait_ge(turned_out, c + 1)
                    if c >= 2:
                        tensor.wait_ge(selfed_out, c - 1)
                    for k in range(n):
                        mm = tensor.matmul(p_self[c % 2][:, k * D:(k + 1) * D], h_t[:, (b + k) * P:(b + k + 1) * P],
                                           self_w[:, :], start=True, stop=True)
                    mm.then_inc(selfed, 1)

                for c, (b, n) in enumerate(CHUNKS):
                    tensor.wait_ge(h_ready, b + n)
                    if c >= 2:
                        tensor.wait_ge(turned_out, c - 1)
                    for k in range(n):
                        mm = tensor.transpose(p_turn[c % 2][:, k * P:(k + 1) * P], h[:, b + k, :], edges.ident[:, :])
                    mm.then_inc(turned, 1)
                    if c >= 1:
                        self_product(c - 1)
                self_product(len(CHUNKS) - 1)
                for i, (q, n) in enumerate(LOTS):
                    tensor.wait_ge(attr_in[i % 2], 16 * (i // 2 + 1))
                    if i >= 2:
                        tensor.wait_ge(bias_out, i - 1)
                    for k in range(n):
                        mm = tensor.matmul(p_bias[i % 2][:, k * 32:(k + 1) * 32], attr[i % 2][:, k, :], we[:, :],
                                           start=True, stop=True)
                    mm.then_inc(bias_made, 1)


def relational_layer(nc, edges, adj, io, dr):
    with Stage(nc, "rel") as st:
        edges.columns(st.ctx, "rel")
        coef = st.sb("coef", [P, BASES, TILES])
        nodes = st.sb("nodes", [P, NODES], F16)
        gathered = st.sb("gathered", [P, GROUP, D])
        index_c = st.sb("index_c", [P, 2, PAIRS_IN_GROUP])
        index = st.sb("index", [P, 2, PAIRS_IN_GROUP], I32)
        src_hot = st.sb("src_hot", [P, 2, SRC_W], BF16)
        dst_hot = st.sb("dst_hot", [P, 2, P], BF16)
        dst_hot_f = st.sb("dst_hot_f", [P, 2, P])
        message = st.sb("message", [P, 2, BASES, D])
        adj_rows = st.sb("adj_rows", [P, SRC_W], BF16)
        agg_t = st.sb("agg_t", [P, BASES, P])
        bases = st.sb("bases", [D, BASES, D])
        x_block = st.sb("x_block", [P, D])
        p_adj = st.ps("p_adj", [P, 7 * BANK])
        p_turn = st.ps("p_turn", [P, 2 * BANK], BF16)
        AGG = 6 * BANK + P
        p_out = p_adj[:, 3 * BANK:3 * BANK + D]

        nodes_ready, w_in, columns_in = st.sem("nodes_ready"), st.sem("w_in"), st.sem("columns_in")
        index_step = st.sem("index_step")
        in_slot = [st.sem(f"in_slot{q}") for q in range(PAIRS_IN_GROUP)]
        gather_go = st.sem("gather_go")
        pairs_gathered = st.sem("pairs_gathered")
        pairs_free = st.sem("pairs_free")
        slots_free = st.sem("slots_free")
        hot_ready = st.sem("hot_ready")
        hot_pre = st.sem("hot_pre")
        message_ready = st.sem("message_ready")
        rows_a, rows_v = st.sem("rows_a"), st.sem("rows_v")
        turned, summed = st.sem("turned"), st.sem("summed")
        adj_a, adj_v = st.sem("adj_a"), st.sem("adj_v")
        x_in, x_summed, x_out = st.sem("x_in"), st.sem("x_summed"), st.sem("x_out")
        adj_clear = st.sem("adj_clear")

        with nc.Block() as block:
            @block.sync
            def _(sync):
                sync.dma_start(edges.src[:, :], dr["src"]).then_inc(columns_in, 16)
                sync.dma_start(edges.dst[:, :], dr["dst"]).then_inc(columns_in, 16)
                sync.dma_start(bases[:, :, :], io["bases"].rearrange("b i o -> i b o")).then_inc(w_in, 16)
                sync.dma_start(coef[:, :, :], dr["coef"]).then_inc(w_in, 16)
                with sync.Fori(0, GROUPS) as g:
                    for q in range(PAIRS_IN_GROUP):
                        sync.wait_ge(in_slot[q], 32 * g + 32)
                        sync.sem_inc(pairs_gathered, 1)

            @block.gpsimd
            def _(gpsimd):
                gpsimd.iota(nodes[:, :], pattern=[[1, NODES]], base=-CENTER, channel_multiplier=0,
                            allow_small_or_imprecise_dtypes=True).then_inc(nodes_ready, 1)
                gpsimd.wait_ge(nodes_ready, 1)
                gpsimd.wait_ge(columns_in, 32)
                gpsimd.sem_inc(pairs_free, PAIRS_IN_GROUP)
                with gpsimd.Fori(0, GROUPS) as g:
                    for half in range(2):
                        gpsimd.wait_ge(pairs_free, PAIRS_IN_GROUP * g + 4 * half + 4)
                        gpsimd.sem_inc(gather_go, 1)
                        gpsimd.tensor_copy(index_c[:, half, :], edges.src[:, bass.ds(g * GROUP + half * 8, 8)])\
                              .then_inc(index_step, 1)
                        gpsimd.wait_ge(index_step, 4 * g + 2 * half + 1)
                        gpsimd.sem_inc(gather_go, 1)
                        gpsimd.tensor_scalar(index[:, half, :], index_c[:, half, :], float(CENTER), None, ALU.add)\
                              .then_inc(index_step, 1)
                        gpsimd.wait_ge(index_step, 4 * g + 2 * half + 2)
                        gpsimd.sem_inc(gather_go, 1)
                        for q in range(4 * half, 4 * half + 4):
                            for k in range(2):
                                gpsimd.indirect_dma_start(
                                    out=gathered[:, 2 * q + k, :], out_offset=None, in_=dr["h0"],
                                    in_offset=bass.IndirectOffsetOnAxis(
                                        ap=index[:, half, (2 * q + k) % 8:(2 * q + k) % 8 + 1], axis=0))\
                                    .then_inc(in_slot[q], 16)

            @block.vector
            def _(vector):
                vector.memset(adj[P // 2:P, BLOCKS - 1, :], 0.0)
                vector.wait_ge(nodes_ready, 1)
                vector.wait_ge(columns_in, 32)

                def one_hots(b, p):
                    for k in range(2):
                        vector.wait_ge(slots_free, 2 * p + 2 * b + k + 1)
                        dst = edges.dst[:, bass.ds(2 * p + k, 1)]
                        vector.tensor_scalar(src_hot[:, k, :], nodes[:, 0:SRC_W], edges.src[:, bass.ds(2 * p + k, 1)],
                                             None, ALU.is_equal).then_inc(hot_pre, 1)
                        vector.tensor_scalar(dst_hot[:, k, :], nodes[:, bass.ds(b * P, P)], dst, None,
                                             ALU.is_equal).then_inc(hot_pre, 1)
                        vector.tensor_scalar(dst_hot_f[:, k, :], nodes[:, bass.ds(b * P, P)], dst, None,
                                             ALU.is_equal).then_inc(hot_ready, 1)

                with vector.Fori(0, BLOCKS) as b:
                    first = vector.value_load(edges.first_pair[0:1, bass.ds(b, 1)], min_val=0, max_val=PAIRS - 1)
                    last = vector.value_load(edges.first_pair[0:1, bass.ds(b + 1, 1)], min_val=0, max_val=PAIRS - 1)
                    one_hots(b, first)
                    with vector.If(last > first):
                        with vector.Fori(first + 1, last + 1) as p:
                            one_hots(b, p)
                    vector.wait_ge(slots_free, 2 * last + 2 * b + 4)
                    vector.tensor_copy(adj_rows[:, 3 * BANK:SRC_W], p_adj[:, 3 * BANK:SRC_W]).then_inc(rows_v, 1)
                    vector.tensor_copy(agg_t[:, :, :], p_adj[:, AGG:AGG + BASES * P].rearrange("p (a d) -> p a d", d=P))\
                          .then_inc(rows_v, 1)
                    columns = bass.ds(b * P, P)
                    vector.wait_ge(turned, 4 * b + 2)
                    vector.tensor_copy(adj[:, 8:16, columns], p_adj[:, 0:BANK].bitcast(BF16)
                                       .rearrange("p (k d) -> p k d", d=P)).then_inc(adj_v, 1)
                    vector.wait_ge(turned, 4 * b + 4)
                    vector.tensor_copy(adj[0:P // 2, 24, columns], p_adj[0:P // 2, 2 * BANK:2 * BANK + P // 2]
                                       .bitcast(BF16)).then_inc(adj_v, 1)
                    vector.wait_ge(summed, b + 1)
                    vector.wait_ge(x_in, 16 * b + 16)
                    vector.tensor_tensor(x_block[:, :], x_block[:, :], p_out, ALU.add).then_inc(x_summed, 1)

            @block.scalar
            def _(scalar):
                scalar.wait_ge(w_in, 32)

                def messages(b, p, release):
                    slot = (p % PAIRS_IN_GROUP) * 2
                    scalar.wait_ge(pairs_gathered, p + 1)
                    for k in range(2):
                        scalar.wait_ge(slots_free, 2 * p + 2 * b + k + 1)
                        for a in range(BASES):
                            m = scalar.activation(message[:, k, a, :], gathered[:, bass.ds(slot + k, 1), :], ACT.Copy,
                                                  scale=coef[:, a, bass.ds(2 * p + k, 1)])
                            if a == 1:
                                m.then_inc(message_ready, 1)
                            elif k == 0 and release:
                                m.then_inc(pairs_free, 1)

                with scalar.Fori(0, BLOCKS) as b:
                    first = scalar.value_load(edges.first_pair[0:1, bass.ds(b, 1)], min_val=0, max_val=PAIRS - 1)
                    last = scalar.value_load(edges.first_pair[0:1, bass.ds(b + 1, 1)], min_val=0, max_val=PAIRS - 1)
                    messages(b, first, False)
                    with scalar.If(last > first):
                        with scalar.Fori(first + 1, last + 1) as p:
                            messages(b, p, True)
                    scalar.wait_ge(slots_free, 2 * last + 2 * b + 4)
                    scalar.activation(adj_rows[:, 0:3 * BANK], p_adj[:, 0:3 * BANK], ACT.Copy).then_inc(rows_a, 1)
                    columns = bass.ds(b * P, P)
                    scalar.wait_ge(turned, 4 * b + 1)
                    scalar.activation(adj[:, 0:8, columns], p_turn[:, :].rearrange("p (k d) -> p k d", d=P),
                                      ACT.Copy).then_inc(adj_a, 1)
                    scalar.wait_ge(turned, 4 * b + 3)
                    scalar.activation(adj[:, 16:24, columns], p_adj[:, BANK:2 * BANK].bitcast(BF16)
                                      .rearrange("p (k d) -> p k d", d=P), ACT.Copy).then_inc(adj_a, 1)
                    scalar.dma_start(x_block[:, :], dr["x0"][bass.ds(b * P, P), :]).then_inc(x_in, 16)
                    scalar.wait_ge(x_summed, b + 1)
                    scalar.dma_start(dr["x1"][bass.ds(b * P, P), :], x_block[:, :]).then_inc(x_out, 16)
                    scalar.wait_ge(x_out, 16 * b + 16)

            @block.tensor
            def _(tensor):
                tensor.sem_inc(slots_free, 2)

                def sums(b, p, start):
                    for k in range(2):
                        tensor.wait_ge(hot_ready, 2 * p + 2 * b + k + 1)
                        tensor.wait_ge(message_ready, 2 * p + 2 * b + k + 1)
                        begin = start and k == 0
                        for j in range(7):
                            a, z = j * BANK, min((j + 1) * BANK, SRC_W)
                            tensor.matmul(p_adj[:, a:z], dst_hot[:, k, :], src_hot[:, k, a:z],
                                          start=begin, stop=True, skip_group_check=True)
                        for a in range(BASES):
                            mm = tensor.matmul(p_adj[:, AGG + a * P:AGG + (a + 1) * P], message[:, k, a, :],
                                               dst_hot_f[:, k, :], start=False, stop=True, skip_group_check=True)
                        mm.then_inc(slots_free, 1)

                with tensor.Fori(0, BLOCKS) as b:
                    first = tensor.value_load(edges.first_pair[0:1, bass.ds(b, 1)], min_val=0, max_val=PAIRS - 1)
                    last = tensor.value_load(edges.first_pair[0:1, bass.ds(b + 1, 1)], min_val=0, max_val=PAIRS - 1)
                    sums(b, first, True)
                    with tensor.If(last > first):
                        with tensor.Fori(first + 1, last + 1) as p:
                            sums(b, p, False)
                    tensor.wait_ge(rows_a, b + 1)
                    tensor.wait_ge(rows_v, 2 * b + 2)
                    for r in range(3):
                        for k in range(8):
                            to = p_turn[:, k * P:(k + 1) * P] if r == 0 else \
                                p_adj[:, (r - 1) * BANK + k * P // 2:(r - 1) * BANK + (k + 1) * P // 2].bitcast(BF16)
                            mm = tensor.transpose(to, adj_rows[:, (8 * r + k) * P:(8 * r + k + 1) * P],
                                                  edges.ident16[:, :])
                        mm.then_inc(turned, 1)
                    tensor.transpose(p_adj[0:P // 2, 2 * BANK:2 * BANK + P // 2].bitcast(BF16),
                                     adj_rows[:, 24 * P:SRC_W], edges.ident16[:, :]).then_inc(turned, 1)
                    for a in range(BASES):
                        mm = tensor.matmul(p_out, agg_t[:, a, :], bases[:, a, :], start=(a == 0), stop=(a == 1))
                    mm.then_inc(summed, 1)
                    tensor.wait_ge(adj_a, 2 * b + 2)
                    tensor.wait_ge(adj_v, 2 * b + 2)
                    tensor.wait_ge(x_summed, b + 1)


def split_vector(vector, source, parts, rest, cols, i, hi_ready, rest_ready, mid_ready, split_done):
    vector.wait_ge(hi_ready, i + 1)
    vector.tensor_tensor(rest, source, parts[:, 0, cols], ALU.subtract).then_inc(rest_ready, 1)
    vector.wait_ge(mid_ready, i + 1)
    vector.wait_ge(rest_ready, i + 1)
    vector.tensor_tensor(parts[:, 2, cols], rest, parts[:, 1, cols], ALU.subtract).then_inc(split_done, 1)


def aggregate(tensor, p_agg, parts, adj, cols):
    def source_block(k, start):
        for i in range(3):
            mm = tensor.matmul(p_agg, parts[:, i, bass.ds(k * P, P)], adj[:, bass.ds(k, 1), cols],
                               start=start and i == 0, stop=True, skip_group_check=True)
        return mm
    source_block(0, True)
    with tensor.Fori(1, BLOCKS - 1) as k:
        source_block(k, False)
    return source_block(BLOCKS - 1, False)


def enter_gated(nc, ident, state, parts, io, dr):
    with Stage(nc, "enter") as st:
        x = st.sb("x", [P, BLOCKS, D])
        lin_w = st.sb("lin_w", [D, D])
        lin_b = st.sb("lin_b", [D, 1])
        ln = NormBuffers(st)
        h = state[:, :].rearrange("p (k f) -> p k f", f=D)
        h_t = parts[:, :, :].rearrange("p i n -> p (i n)").bitcast(F32)
        p_turn = [st.ps(f"p_turn{i}", [P, BANK]) for i in range(2)]
        p_lin = [st.ps(f"p_lin{i}", [P, BANK]) for i in range(2)]
        x_in, w_in, h_ready = st.sem("x_in"), st.sem("w_in"), st.sem("h_ready")
        turned, turned_out, linear, linear_out = (st.sem(n) for n in ("turned", "turned_out", "linear", "linear_out"))
        with nc.Block() as block:
            @block.sync
            def _(sync):
                sync.dma_start(x[:, :, :], rows(dr["x1"])).then_inc(x_in, 16)
                sync.dma_start(lin_w[:, :], io["lin_w"]).then_inc(w_in, 16)
                sync.dma_start(lin_b[:, :], io["lin_b"]).then_inc(w_in, 16)

            @block.vector
            def _(vector):
                vector.wait_ge(x_in, 16)
                norm_vector(vector, ln, x)
                for c, (b, n) in enumerate(CHUNKS):
                    vector.wait_ge(turned, c + 1)
                    vector.tensor_copy(h_t[:, b * P:(b + n) * P], p_turn[c % 2][:, 0:n * P]).then_inc(turned_out, 1)

            @block.scalar
            def _(scalar):
                norm_scalar(scalar, ln, x, h, h_ready)
                scalar.wait_ge(w_in, 32)
                for c, (b, n) in enumerate(CHUNKS):
                    scalar.wait_ge(linear, c + 1)
                    scalar.activation(state[:, b * P:(b + n) * P], p_lin[c % 2][:, 0:n * P], ACT.Identity,
                                      bias=lin_b[:, 0:1]).then_inc(linear_out, 1)

            @block.tensor
            def _(tensor):
                tensor.wait_ge(w_in, 32)

                def linear_product(c):
                    b, n = CHUNKS[c]
                    tensor.wait_ge(turned_out, c + 1)
                    if c >= 2:
                        tensor.wait_ge(linear_out, c - 1)
                    tensor.matmul(p_lin[c % 2][:, 0:n * P], lin_w[:, :], h_t[:, b * P:(b + n) * P],
                                  start=True, stop=True).then_inc(linear, 1)

                for c, (b, n) in enumerate(CHUNKS):
                    tensor.wait_ge(h_ready, b + n)
                    if c >= 2:
                        tensor.wait_ge(turned_out, c - 1)
                    for k in range(n):
                        mm = tensor.transpose(p_turn[c % 2][:, k * P:(k + 1) * P], h[:, b + k, :], ident[:, :])
                    mm.then_inc(turned, 1)
                    if c >= 1:
                        linear_product(c - 1)
                linear_product(len(CHUNKS) - 1)


def gated_layers(nc, adj, state, parts, io):
    C = len(CHUNKS)
    LAYERS = 3
    with Stage(nc, "gated") as st:
        weight = st.sb("weight", [D, D])
        w_ih = st.sb("w_ih", [D, 3 * D])
        w_hh = st.sb("w_hh", [D, 3 * D])
        b_ih = st.sb("b_ih", [D, 3])
        b_hh = st.sb("b_hh", [D, 3])
        b_rz = st.sb("b_rz", [D, 2])
        agg = [st.sb(f"agg{i}", [P, BANK]) for i in range(2)]
        gate_r, gate_z, mix, delta = (st.sb(n, [P, BANK]) for n in ("gate_r", "gate_z", "mix", "delta"))
        rest = [gate_r, gate_z]
        new = gate_r
        p_m = [st.ps(f"p_m{i}", [P, BANK]) for i in range(2)]
        p_agg = [st.ps(f"p_agg{i}", [P, BANK]) for i in range(2)]
        p_r, p_z, p_in, p_hn = (st.ps(n, [P, BANK]) for n in ("p_r", "p_z", "p_in", "p_hn"))
        names = ("weight_in", "gates_in", "bias_ready", "m_made", "hi_ready", "rest_ready", "mid_ready",
                 "split_done", "agg_made", "agg_ready", "gates_made", "r_ready", "z_ready", "mix_step",
                 "new_ready", "h_step", "h_new")
        (weight_in, gates_in, bias_ready, m_made, hi_ready, rest_ready, mid_ready, split_done, agg_made,
         agg_ready, gates_made, r_ready, z_ready, mix_step, new_ready, h_step, h_new) = (st.sem(n) for n in names)

        with nc.Block() as block:
            @block.sync
            def _(sync):
                sync.dma_start(w_ih[:, :], io["w_ih"]).then_inc(gates_in, 16)
                sync.dma_start(w_hh[:, :], io["w_hh"]).then_inc(gates_in, 16)
                sync.dma_start(b_ih[:, :], io["b_ih"]).then_inc(gates_in, 16)
                sync.dma_start(b_hh[:, :], io["b_hh"]).then_inc(gates_in, 16)
                sync.dma_start(weight[:, :], io["layer_w"][0]).then_inc(weight_in, 16)
                for layer in range(1, LAYERS):
                    sync.wait_ge(m_made, C * layer)
                    sync.dma_start(weight[:, :], io["layer_w"][layer]).then_inc(weight_in, 16)

            @block.vector
            def _(vector):
                vector.wait_ge(gates_in, 64)
                vector.tensor_tensor(b_rz[:, :], b_ih[:, 0:2], b_hh[:, 0:2], ALU.add).then_inc(bias_ready, 1)
                with vector.Fori(0, LAYERS) as layer:
                    for c, (b, n) in enumerate(CHUNKS):
                        if c >= 2:
                            vector.wait_ge(split_done, layer * C + c - 1)
                        cols = slice(b * P, (b + n) * P)
                        split_vector(vector, p_m[c % 2][:, 0:n * P], parts, rest[c % 2][:, 0:n * P], cols,
                                     layer * C + c, hi_ready, rest_ready, mid_ready, split_done)
                    for c, (b, n) in enumerate(CHUNKS):
                        w, i = n * P, layer * C + c
                        h = state[:, b * P:b * P + w]
                        vector.wait_ge(r_ready, i + 1)
                        vector.scalar_tensor_tensor(mix[:, 0:w], p_hn[:, 0:w], b_hh[:, 2:3], gate_r[:, 0:w],
                                                    ALU.add, ALU.mult).then_inc(mix_step, 1)
                        vector.wait_ge(mix_step, 2 * i + 1)
                        vector.tensor_tensor(mix[:, 0:w], mix[:, 0:w], p_in[:, 0:w], ALU.add).then_inc(mix_step, 1)
                        vector.wait_ge(new_ready, i + 1)
                        vector.tensor_tensor(delta[:, 0:w], h, new[:, 0:w], ALU.subtract).then_inc(h_step, 1)
                        vector.wait_ge(z_ready, i + 1)
                        vector.wait_ge(h_step, 2 * i + 1)
                        vector.tensor_tensor(delta[:, 0:w], delta[:, 0:w], gate_z[:, 0:w], ALU.mult)\
                              .then_inc(h_step, 1)
                        vector.wait_ge(h_step, 2 * i + 2)
                        vector.tensor_tensor(h, new[:, 0:w], delta[:, 0:w], ALU.add).then_inc(h_new, 1)
                    vector.wait_ge(h_new, layer * C + C)

            @block.scalar
            def _(scalar):
                scalar.wait_ge(bias_ready, 1)
                scalar.wait_ge(gates_in, 64)

                def sums_out(i, c):
                    w = CHUNKS[c][1] * P
                    scalar.wait_ge(agg_made, i + 1)
                    scalar.activation(agg[c % 2][:, 0:w], p_agg[c % 2][:, 0:w], ACT.Copy).then_inc(agg_ready, 1)

                def gates_out(i, c):
                    w = CHUNKS[c][1] * P
                    scalar.wait_ge(gates_made, i + 1)
                    scalar.activation(gate_r[:, 0:w], p_r[:, 0:w], ACT.Sigmoid, bias=b_rz[:, 0:1])\
                          .then_inc(r_ready, 1)
                    scalar.activation(gate_z[:, 0:w], p_z[:, 0:w], ACT.Sigmoid, bias=b_rz[:, 1:2])\
                          .then_inc(z_ready, 1)
                    scalar.wait_ge(mix_step, 2 * i + 2)
                    scalar.activation(new[:, 0:w], mix[:, 0:w], ACT.Tanh, bias=b_ih[:, 2:3]).then_inc(new_ready, 1)

                with scalar.Fori(0, LAYERS) as layer:
                    for c, (b, n) in enumerate(CHUNKS):
                        i, cols = layer * C + c, slice(b * P, (b + n) * P)
                        scalar.wait_ge(m_made, i + 1)
                        scalar.activation(parts[:, 0, cols], p_m[c % 2][:, 0:n * P], ACT.Copy).then_inc(hi_ready, 1)
                        scalar.wait_ge(rest_ready, i + 1)
                        scalar.activation(parts[:, 1, cols], rest[c % 2][:, 0:n * P], ACT.Copy).then_inc(mid_ready, 1)
                    scalar.wait_ge(split_done, layer * C + C)
                    sums_out(layer * C, 0)
                    for c in range(C):
                        if c + 1 < C:
                            sums_out(layer * C + c + 1, c + 1)
                        if c >= 1:
                            scalar.wait_ge(h_new, layer * C + c)
                        gates_out(layer * C + c, c)

            @block.tensor
            def _(tensor):
                tensor.wait_ge(gates_in, 64)

                def sums(layer, c):
                    b, n = CHUNKS[c]
                    if c >= 2:
                        tensor.wait_ge(agg_ready, layer * C + c - 1)
                    aggregate(tensor, p_agg[c % 2][:, 0:n * P], parts, adj, slice(b * P, (b + n) * P))\
                        .then_inc(agg_made, 1)

                def gates(layer, c):
                    b, n = CHUNKS[c]
                    w, i = n * P, layer * C + c
                    h = state[:, b * P:b * P + w]
                    tensor.wait_ge(agg_ready, i + 1)
                    if c >= 1:
                        tensor.wait_ge(h_new, i)
                    for g, out in enumerate((p_r, p_z)):
                        tensor.matmul(out[:, 0:w], w_hh[:, g * D:(g + 1) * D], h, start=True, stop=False)
                        tensor.matmul(out[:, 0:w], w_ih[:, g * D:(g + 1) * D], agg[c % 2][:, 0:w], start=False, stop=True)
                    tensor.matmul(p_hn[:, 0:w], w_hh[:, 2 * D:3 * D], h, start=True, stop=True)
                    tensor.matmul(p_in[:, 0:w], w_ih[:, 2 * D:3 * D], agg[c % 2][:, 0:w], start=True, stop=True)\
                          .then_inc(gates_made, 1)

                with tensor.Fori(0, LAYERS) as layer:
                    tensor.wait_ge(weight_in, layer * 16 + 16)
                    for c, (b, n) in enumerate(CHUNKS):
                        if c >= 2:
                            tensor.wait_ge(split_done, layer * C + c - 1)
                        for k in range(n):
                            mm = tensor.matmul(p_m[c % 2][:, k * D:(k + 1) * D],
                                               state[:, (b + k) * P:(b + k + 1) * P], weight[:, :],
                                               start=True, stop=True)
                        mm.then_inc(m_made, 1)
                    tensor.wait_ge(split_done, layer * C + C)
                    sums(layer, 0)
                    for c in range(C):
                        if c + 1 < C:
                            sums(layer, c + 1)
                        gates(layer, c)
                    tensor.wait_ge(h_new, layer * C + C)


def neighbour_layer(nc, ident, adj, state, parts, io, dr):
    C = len(CHUNKS)
    with Stage(nc, "neigh") as st:
        x = st.sb("x", [P, BLOCKS, D])
        w = st.sb("w", [D, D])
        bias = st.sb("bias", [P, D])
        ones = st.sb("ones", [P, 1])
        total = st.sb("total", [D, 1])
        others = st.sb("others", [P, BANK])
        square = st.sb("square", [P, BANK])
        length = st.sb("length", [P, BLOCKS])
        inverse = st.sb("inverse", [P, BLOCKS])
        ln = NormBuffers(st)
        rest = square
        h = state[:, :].rearrange("p (k f) -> p k f", f=D)
        p_turn = [st.ps(f"p_turn{i}", [P, BANK]) for i in range(2)]
        p_agg = [st.ps(f"p_agg{i}", [P, BANK]) for i in range(2)]
        p_total, p_out, p_length = (st.ps(n, [P, BANK]) for n in ("p_total", "p_out", "p_length"))
        names = ("x_in", "w_in", "const_ready", "turned", "x_ready", "h_ready", "hi_ready", "rest_ready", "mid_ready",
                 "split_done", "total_made", "total_ready", "agg_made", "others_ready", "square_ready", "out_made",
                 "length_ready", "inverse_step", "x_out_ready", "stored", "bias_added")
        (x_in, w_in, const_ready, turned, x_ready, h_ready, hi_ready, rest_ready, mid_ready, split_done,
         total_made, total_ready, agg_made, others_ready, square_ready, out_made, length_ready, inverse_step,
         x_out_ready, stored, bias_added) = (st.sem(n) for n in names)

        with nc.Block() as block:
            @block.sync
            def _(sync):
                sync.dma_start(x[:, :, :], rows(dr["x1"])).then_inc(x_in, 16)
                sync.dma_start(w[:, :], io["neigh_w"]).then_inc(w_in, 16)
                sync.dma_start(bias[:, :], io["neigh_b"].partition_broadcast(P)).then_inc(w_in, 16)
                sync.wait_ge(x_out_ready, BLOCKS)
                sync.dma_start(rows(dr["x3"]), x[:, :, :]).then_inc(stored, 16)
                sync.wait_ge(stored, 16)

            @block.vector
            def _(vector):
                vector.memset(ones[:, :], 1.0).then_inc(const_ready, 1)
                vector.wait_ge(x_in, 16)
                for c, (b, n) in enumerate(CHUNKS):
                    vector.wait_ge(turned, c + 1)
                    vector.tensor_tensor(x[:, b:b + n, :], x[:, b:b + n, :],
                                         p_turn[c % 2][:, 0:n * D].rearrange("p (k f) -> p k f", f=D),
                                         ALU.add).then_inc(x_ready, 1)
                vector.wait_ge(x_ready, C)
                norm_vector(vector, ln, x)
                for c, (b, n) in enumerate(CHUNKS):
                    if c >= 1:
                        vector.wait_ge(split_done, c)
                    split_vector(vector, state[:, b * P:(b + n) * P], parts, rest[:, 0:n * P],
                                 slice(b * P, (b + n) * P), c, hi_ready, rest_ready, mid_ready, split_done)
                vector.wait_ge(w_in, 32)
                vector.tensor_tensor(x[:, :, :], x[:, :, :],
                                     bias[:, :].unsqueeze(1).broadcast_to([P, BLOCKS, D]), ALU.add).then_inc(bias_added, 1)
                vector.wait_ge(total_made, 1)
                vector.tensor_copy(total[:, :], p_total[:, 0:1]).then_inc(total_ready, 1)
                vector.wait_ge(bias_added, 1)
                for c, (b, n) in enumerate(CHUNKS):
                    vector.wait_ge(length_ready, c + 1)
                    vector.tensor_scalar(inverse[:, b:b + n], length[:, b:b + n], 1e-12, None, ALU.max)\
                          .then_inc(inverse_step, 1)
                    vector.wait_ge(inverse_step, 2 * c + 1)
                    vector.reciprocal(inverse[:, b:b + n], inverse[:, b:b + n]).then_inc(inverse_step, 1)
                    vector.wait_ge(inverse_step, 2 * c + 2)
                    for k in range(n):
                        vector.scalar_tensor_tensor(x[:, b + k, :], p_out[:, k * D:(k + 1) * D],
                                                    inverse[:, b + k:b + k + 1], x[:, b + k, :],
                                                    ALU.mult, ALU.add).then_inc(x_out_ready, 1)

            @block.scalar
            def _(scalar):
                scalar.wait_ge(turned, C)
                norm_scalar(scalar, ln, x, h, h_ready)
                scalar.wait_ge(h_ready, BLOCKS)
                for c, (b, n) in enumerate(CHUNKS):
                    cols = slice(b * P, (b + n) * P)
                    scalar.activation(parts[:, 0, cols], state[:, cols], ACT.Copy).then_inc(hi_ready, 1)
                    scalar.wait_ge(rest_ready, c + 1)
                    scalar.activation(parts[:, 1, cols], rest[:, 0:n * P], ACT.Copy).then_inc(mid_ready, 1)
                scalar.wait_ge(total_ready, 1)
                scalar.wait_ge(split_done, C)
                for c, (b, n) in enumerate(CHUNKS):
                    wide = n * P
                    scalar.wait_ge(agg_made, c + 1)
                    if c >= 1:
                        scalar.wait_ge(out_made, c)
                    scalar.activation(others[:, 0:wide], p_agg[c % 2][:, 0:wide], ACT.Identity,
                                      bias=total[:, 0:1], scale=-1.0).then_inc(others_ready, 1)
                    scalar.wait_ge(others_ready, c + 1)
                    scalar.activation(square[:, 0:wide], others[:, 0:wide], ACT.Square).then_inc(square_ready, 1)
                    scalar.wait_ge(out_made, c + 1)
                    scalar.activation(length[:, b:b + n], p_length[:, 0:n], ACT.Sqrt).then_inc(length_ready, 1)

            @block.tensor
            def _(tensor):
                for c, (b, n) in enumerate(CHUNKS):
                    if c >= 2:
                        tensor.wait_ge(x_ready, c - 1)
                    for k in range(n):
                        mm = tensor.transpose(p_turn[c % 2][:, k * P:(k + 1) * P],
                                              state[:, (b + k) * P:(b + k + 1) * P], ident[:, :])
                    mm.then_inc(turned, 1)
                tensor.wait_ge(const_ready, 1)
                tensor.wait_ge(h_ready, BLOCKS)
                for b in range(BLOCKS):
                    m = P if b < BLOCKS - 1 else LAST_ROWS
                    mm = tensor.matmul(p_total[:, 0:1], state[0:m, b * P:(b + 1) * P], ones[0:m, :],
                                       start=(b == 0), stop=(b == BLOCKS - 1))
                mm.then_inc(total_made, 1)
                tensor.wait_ge(split_done, C)
                tensor.wait_ge(w_in, 32)

                def sums(c):
                    b, n = CHUNKS[c]
                    if c >= 2:
                        tensor.wait_ge(others_ready, c - 1)
                    aggregate(tensor, p_agg[c % 2][:, 0:n * P], parts, adj, slice(b * P, (b + n) * P))\
                        .then_inc(agg_made, 1)

                sums(0)
                for c, (b, n) in enumerate(CHUNKS):
                    if c + 1 < C:
                        sums(c + 1)
                    tensor.wait_ge(square_ready, c + 1)
                    if c >= 1:
                        tensor.wait_ge(x_out_ready, CHUNKS[c][0])
                        tensor.wait_ge(length_ready, c)
                    for k in range(n):
                        tensor.matmul(p_out[:, k * D:(k + 1) * D], others[:, k * P:(k + 1) * P], w[:, :],
                                      start=True, stop=True)
                        mm = tensor.matmul(p_length[:, k:k + 1], square[:, k * P:(k + 1) * P], ones[:, :],
                                           start=True, stop=True)
                    mm.then_inc(out_made, 1)


def attention_tables(nc, ident, io, dr):
    C, W = len(CHUNKS), 3 * D
    with Stage(nc, "tables") as st:
        x = st.sb("x", [P, BLOCKS, D])
        h = st.sb("h", [P, BLOCKS, D])
        h_t = st.sb("h_t", [P, NODES])
        w_kvq = st.sb("w_kvq", [D, W])
        b_kvq = st.sb("b_kvq", [P, W])
        kvq = st.sb("kvq", [P, BLOCKS, W])
        ln = NormBuffers(st)
        p_turn = [st.ps(f"p_turn{i}", [P, BANK]) for i in range(2)]
        p_kvq = [st.ps(f"p_kvq{i}", [P, BANK]) for i in range(4)]
        names = ("x_in", "w_in", "h_ready", "turned", "turned_out", "scaled", "made", "made_out", "stored")
        x_in, w_in, h_ready, turned, turned_out, scaled, made, made_out, stored = (st.sem(n) for n in names)
        with nc.Block() as block:
            @block.sync
            def _(sync):
                sync.dma_start(x[:, :, :], rows(dr["x3"])).then_inc(x_in, 16)
                for i, n in enumerate(("k", "v", "q")):
                    sync.dma_start(w_kvq[:, i * D:(i + 1) * D], io["w" + n]).then_inc(w_in, 16)
                    sync.dma_start(b_kvq[:, i * D:(i + 1) * D], io["b" + n].partition_broadcast(P)).then_inc(w_in, 16)
                sync.wait_ge(made_out, BLOCKS)
                sync.dma_start(rows(dr["kv"]), kvq[:, :, 0:2 * D]).then_inc(stored, 16)
                sync.dma_start(rows(dr["q"]), kvq[:, :, 2 * D:W]).then_inc(stored, 16)
                sync.wait_ge(stored, 32)

            @block.vector
            def _(vector):
                vector.wait_ge(w_in, 96)
                for t in (w_kvq, b_kvq):
                    vector.tensor_scalar(t[:, 2 * D:W], t[:, 2 * D:W], HEAD_DIM ** -0.5, None, ALU.mult)\
                          .then_inc(scaled, 1)
                vector.wait_ge(x_in, 16)
                norm_vector(vector, ln, x)
                vector.wait_ge(scaled, 2)
                for b in range(BLOCKS):
                    vector.wait_ge(made, b + 1)
                    vector.tensor_tensor(kvq[:, b, :], p_kvq[b % 4][:, 0:W], b_kvq[:, :], ALU.add).then_inc(made_out, 1)

            @block.scalar
            def _(scalar):
                norm_scalar(scalar, ln, x, h, h_ready)
                for c, (b, n) in enumerate(CHUNKS):
                    scalar.wait_ge(turned, c + 1)
                    scalar.activation(h_t[:, b * P:(b + n) * P], p_turn[c % 2][:, 0:n * P], ACT.Copy)\
                          .then_inc(turned_out, 1)

            @block.tensor
            def _(tensor):
                tensor.wait_ge(scaled, 2)

                def products(c):
                    b0, n = CHUNKS[c]
                    tensor.wait_ge(turned_out, c + 1)
                    for b in range(b0, b0 + n):
                        if b >= 4:
                            tensor.wait_ge(made_out, b - 3)
                        tensor.matmul(p_kvq[b % 4][:, 0:W], h_t[:, b * P:(b + 1) * P], w_kvq[:, :],
                                      start=True, stop=True).then_inc(made, 1)

                for c, (b, n) in enumerate(CHUNKS):
                    tensor.wait_ge(h_ready, b + n)
                    if c >= 2:
                        tensor.wait_ge(turned_out, c - 1)
                    for k in range(n):
                        mm = tensor.transpose(p_turn[c % 2][:, k * P:(k + 1) * P], h[:, b + k, :], ident[:, :])
                    mm.then_inc(turned, 1)
                    if c >= 1:
                        products(c - 1)
                products(C - 1)


def block_range(engine, edges, b):
    return [engine.value_load(edges.first_pair[0:1, bass.ds(i, 1)], min_val=0, max_val=PAIRS - 1) for i in (b, b + 1)]


def edge_scores(nc, edges, score, dr):
    with Stage(nc, "score") as st:
        nodes = st.sb("nodes", [P, NODES], F16)
        gathered = st.sb("gathered", [P, GROUP, 2 * D])
        source = st.sb("source", [P, TILES], I32)
        index = st.sb("index", [P, 2, PAIRS_IN_GROUP], I32)
        query = st.sb("query", [P, BLOCKS, D])
        dst_hot = st.sb("dst_hot", [P, 2, P], BF16)
        hot_t = st.sb("hot_t", [P, 2, P])
        product = st.sb("product", [P, 2, D])
        dots = st.sb("dots", [P, 2, HEADS])
        p_hot = st.ps("p_hot", [P, 2 * BANK], BF16)
        p_query = st.ps("p_query", [P, BANK])
        names = ("columns_in", "nodes_ready", "source_ready", "tables_in", "index_step", "gather_go", "pairs_gathered", "pairs_free",
                 "pairs_stored", "hot_ready", "turned", "hot_t_ready", "query_ready", "product_ready", "dots_ready",
                 "score_added")
        (columns_in, nodes_ready, source_ready, tables_in, index_step, gather_go, pairs_gathered, pairs_free,
         pairs_stored, hot_ready, turned, hot_t_ready, query_ready, product_ready, dots_ready,
         score_added) = (st.sem(n) for n in names)
        in_slot = [st.sem(f"in_slot{q}") for q in range(PAIRS_IN_GROUP)]
        values_out = [st.sem(f"values_out{q}") for q in range(PAIRS_IN_GROUP)]

        with nc.Block() as block:
            @block.sync
            def _(sync):
                sync.dma_start(edges.src[:, :], dr["src"]).then_inc(columns_in, 16)
                sync.dma_start(edges.dst[:, :], dr["dst"]).then_inc(columns_in, 16)
                sync.dma_start(query[:, :, :], rows(dr["q"])).then_inc(tables_in, 16)
                sync.dma_start(score[:, :, :, :].rearrange("p g h t -> p (g h t)"), dr["bias"]).then_inc(tables_in, 16)
                with sync.Fori(0, GROUPS) as g:
                    for q in range(PAIRS_IN_GROUP + 3):
                        if q < PAIRS_IN_GROUP:
                            sync.wait_ge(in_slot[q], 32 * g + 32)
                            sync.sem_inc(pairs_gathered, 1)
                            sync.dma_start(dr["values"][:, bass.ds(g * GROUP + 2 * q, 2), :],
                                           gathered[:, 2 * q:2 * q + 2, D:2 * D]).then_inc(values_out[q], 16)
                        if q >= 3:
                            sync.wait_ge(values_out[q - 3], 16 * g + 16)
                            sync.sem_inc(pairs_stored, 1)

            @block.gpsimd
            def _(gpsimd):
                gpsimd.iota(nodes[:, :], pattern=[[1, NODES]], base=-CENTER, channel_multiplier=0,
                            allow_small_or_imprecise_dtypes=True).then_inc(nodes_ready, 1)
                gpsimd.sem_inc(pairs_free, PAIRS_IN_GROUP)
                gpsimd.sem_inc(pairs_stored, PAIRS_IN_GROUP)
                gpsimd.wait_ge(nodes_ready, 1)
                gpsimd.wait_ge(source_ready, 1)
                with gpsimd.Fori(0, GROUPS) as g:
                    for half in range(2):
                        gpsimd.wait_ge(pairs_stored, PAIRS_IN_GROUP * g + 4 * half + 4)
                        gpsimd.sem_inc(gather_go, 1)
                        gpsimd.wait_ge(pairs_free, PAIRS_IN_GROUP * g + 4 * half + 4)
                        gpsimd.sem_inc(gather_go, 1)
                        gpsimd.tensor_copy(index[:, half, :], source[:, bass.ds(g * GROUP + half * 8, 8)])\
                              .then_inc(index_step, 1)
                        gpsimd.wait_ge(index_step, 2 * g + half + 1)
                        gpsimd.sem_inc(gather_go, 1)
                        for q in range(4 * half, 4 * half + 4):
                            for k in range(2):
                                i = (2 * q + k) % 8
                                gpsimd.indirect_dma_start(
                                    out=gathered[:, 2 * q + k, :], out_offset=None, in_=dr["kv"],
                                    in_offset=bass.IndirectOffsetOnAxis(ap=index[:, half, i:i + 1], axis=0))\
                                    .then_inc(in_slot[q], 16)

            @block.vector
            def _(vector):
                vector.wait_ge(columns_in, 32)
                vector.tensor_scalar(source[:, :], edges.src[:, :], float(CENTER), None, ALU.add)\
                      .then_inc(source_ready, 1)
                vector.wait_ge(nodes_ready, 1)
                vector.wait_ge(tables_in, 32)
                vector.sem_inc(score_added, 1)

                def dot(b, p):
                    step = p + b
                    for k in range(2):
                        vector.tensor_scalar(dst_hot[:, k, :], nodes[:, bass.ds(b * P, P)],
                                             edges.dst[:, bass.ds(2 * p + k, 1)], None,
                                             ALU.is_equal).then_inc(hot_ready, 1)
                    vector.wait_ge(pairs_gathered, p + 1)
                    vector.wait_ge(query_ready, step + 1)
                    slot = (p % PAIRS_IN_GROUP) * 2
                    vector.tensor_tensor(product[:, :, :], gathered[:, bass.ds(slot, 2), 0:D],
                                         p_query[:, 0:2 * D].rearrange("p (k f) -> p k f", f=D),
                                         ALU.mult).then_inc(product_ready, 1)
                    vector.wait_ge(product_ready, step + 1)
                    vector.tensor_reduce(dots[:, :, :], product[:, :, :].rearrange("p k (h d) -> p k h d", d=HEAD_DIM),
                                                  AX.X, ALU.add).then_inc(dots_ready, 1)
                    vector.wait_ge(dots_ready, step + 1)
                    vector.wait_ge(score_added, step + 1)
                    here = score[:, bass.ds(p // PAIRS_IN_GROUP, 1), :, bass.ds(slot, 2)].rearrange("p g h t -> p (g h) t")
                    vector.tensor_tensor(here, here, dots[:, :, :].rearrange("p k h -> p h k"), ALU.add)\
                          .then_inc(score_added, 1)

                with vector.Fori(0, BLOCKS) as b:
                    first, last = block_range(vector, edges, b)
                    dot(b, first)
                    with vector.If(last > first):
                        with vector.Fori(first + 1, last + 1) as p:
                            vector.sem_inc(pairs_free, 1)
                            dot(b, p)

            @block.scalar
            def _(scalar):
                with scalar.Fori(0, PAIRS + BLOCKS - 1) as step:
                    scalar.wait_ge(turned, step + 1)
                    scalar.activation(hot_t[:, :, :], p_hot[:, 0:2 * P].rearrange("p (k e) -> p k e", e=P),
                                      ACT.Copy).then_inc(hot_t_ready, 1)

            @block.tensor
            def _(tensor):
                tensor.wait_ge(tables_in, 32)

                def queries(b, p):
                    step = p + b
                    tensor.wait_ge(hot_ready, 2 * step + 2)
                    for k in range(2):
                        mm = tensor.transpose(p_hot[:, k * P:(k + 1) * P], dst_hot[:, k, :], edges.ident16[:, :])
                    mm.then_inc(turned, 1)
                    tensor.wait_ge(hot_t_ready, step + 1)
                    for k in range(2):
                        mm = tensor.matmul(p_query[:, k * D:(k + 1) * D], hot_t[:, k, :], query[:, bass.ds(b, 1), :],
                                           start=True, stop=True)
                    mm.then_inc(query_ready, 1)

                with tensor.Fori(0, BLOCKS) as b:
                    first, last = block_range(tensor, edges, b)
                    queries(b, first)
                    with tensor.If(last > first):
                        with tensor.Fori(first + 1, last + 1) as p:
                            queries(b, p)
                    tensor.wait_ge(query_ready, last + b + 1)


def softmax_weights(nc, edges, score, io, dr):
    SPANS = P // HEADS
    SPAN = EDGES // SPANS
    TURNS = [(g, min(4, GROUPS - g)) for g in range(0, GROUPS, 4)]
    LOW = -1.7e38
    PIECES = 4
    with Stage(nc, "soft") as st:
        turned_rows = st.sb("turned_rows", [P, GROUPS, P])
        dst = st.sb("dst", [P, SPAN + 2], I32)
        same_prev = st.sb("same_prev", [P, SPAN])
        same_next = st.sb("same_next", [P, SPAN])
        line = st.sb("line", [P, SPAN])
        peak = st.sb("peak", [P, SPAN])
        ends = st.sb("ends", [P, 2, 2])
        through = st.sb("through", [1, 2, P])
        carry_row = st.sb("carry_row", [1, 2, P + 1])
        carry = st.sb("carry", [P, 2])
        one = st.sb("one", [1, 1])
        p_turn = [st.ps(f"p_turn{i}", [P, BANK]) for i in range(2)]
        p_ends, p_carry = st.ps("p_ends", [P, BANK]), st.ps("p_carry", [P, BANK])
        names = ("dst_in", "turned", "turned_out", "rows_out", "line_in", "ends_turned", "through_ready",
                 "carry_made", "carry_turned", "shifted", "weights", "line_out", "rows_in", "back", "back_even", "back_out")
        (dst_in, turned, turned_out, rows_out, line_in, ends_turned, through_ready,
         carry_made, carry_turned, shifted, weights, line_out, rows_in, back, back_even, back_out) = (st.sem(n) for n in names)
        v_step = Count(st.sem("v_step"))
        ends_ready = st.sem("ends_ready")
        dram_line = dr["line"]
        by_head = dram_line.rearrange("(h c) e -> h (c e)", h=HEADS).rearrange("h (g t e) -> h t g e", t=GROUP, e=P)

        with nc.Block() as block:
            @block.sync
            def _(sync):
                windows = bass.AP(dr["dst_line"].tensor, 0, [[SPAN, SPANS], [1, SPAN + 2]])
                for h in range(HEADS):
                    sync.dma_start(dst[h * SPANS:(h + 1) * SPANS, :], windows).then_inc(dst_in, 16)
                sync.wait_ge(turned_out, len(TURNS))
                for h in range(HEADS):
                    sync.dma_start(by_head[h], turned_rows[h * GROUP:(h + 1) * GROUP, :, :]).then_inc(rows_out, 16)
                sync.wait_ge(rows_out, 16 * HEADS)
                sync.dma_start(line[:, :], dram_line).then_inc(line_in, 16)
                sync.wait_ge(weights, PIECES)
                sync.dma_start(dram_line, line[:, :]).then_inc(line_out, 16)
                sync.wait_ge(line_out, 16)
                for h in range(HEADS):
                    sync.dma_start(turned_rows[h * GROUP:(h + 1) * GROUP, :, :], by_head[h]).then_inc(rows_in, 16)

            @block.vector
            def _(vector):
                vector.wait_ge(dst_in, 16 * HEADS)
                vector.memset(one[:, :], 1.0).then_inc(v_step.sem, 1)
                vector.memset(carry_row[:, :, :], LOW).then_inc(v_step.sem, 1)
                v_step.up(2)
                for same, other in ((same_prev, 0), (same_next, 2)):
                    vector.tensor_tensor(same[:, :], dst[:, 1:SPAN + 1], dst[:, other:SPAN + other], ALU.is_equal)\
                          .then_inc(v_step.sem, 1)
                    vector.wait_ge(v_step.sem, v_step.up())
                    vector.tensor_scalar(same[:, :], same[:, :], 0.5, -2 * LOW, ALU.subtract, ALU.mult)\
                          .then_inc(v_step.sem, 1)
                    v_step.up()
                vector.wait_ge(v_step.sem, v_step.n)
                vector.tensor_reduce(ends[:, 0, 1:2], same_prev[:, :], AX.X, ALU.min).then_inc(v_step.sem, 1)
                vector.tensor_reduce(ends[:, 1, 1:2], same_next[:, :], AX.X, ALU.min).then_inc(v_step.sem, 1)
                vector.wait_ge(v_step.sem, v_step.up(2))
                vector.wait_ge(line_in, 16)
                for way, same in enumerate((same_prev, same_next)):
                    turn = slice(None) if way == 0 else slice(None, None, -1)
                    last = SPAN - 1 if way == 0 else 0
                    def scan(initial):
                        vector.tensor_tensor_scan(peak[:, turn], same[:, turn], source[:, turn], initial,
                                                  ALU.min, ALU.max).then_inc(v_step.sem, 1)
                        vector.wait_ge(v_step.sem, v_step.up())

                    source = line if way == 0 else turned_rows[:, :, :].rearrange("p g e -> p (g e)")
                    scan(LOW)
                    vector.tensor_copy(ends[:, way, 0:1], peak[:, last:last + 1]).then_inc(ends_ready, 1)
                    vector.wait_ge(ends_turned, way + 1)
                    vector.tensor_copy(through[:, way, :], p_ends[0:1, P:2 * P]).then_inc(v_step.sem, 1)
                    vector.wait_ge(v_step.sem, v_step.up())
                    leaves = carry_row[:, way, 1:P + 1] if way == 0 else carry_row[:, way, 0:P]
                    vector.tensor_tensor_scan(leaves[:, turn], through[:, way, turn], p_ends[0:1, 0:P][:, turn], LOW,
                                              ALU.min, ALU.max).then_inc(carry_made, 1)
                    vector.wait_ge(carry_turned, way + 1)
                    vector.tensor_copy(carry[:, way:way + 1], p_carry[:, 0:1]).then_inc(v_step.sem, 1)
                    vector.wait_ge(v_step.sem, v_step.up())
                    scan(carry[:, way:way + 1])
                    if way == 0:
                        vector.tensor_copy(turned_rows[:, :, :].rearrange("p g e -> p (g e)"), peak[:, :])\
                              .then_inc(v_step.sem, 1)
                        vector.wait_ge(v_step.sem, v_step.up())
                for i in range(PIECES):
                    a, z = SPAN * i // PIECES, SPAN * (i + 1) // PIECES
                    vector.tensor_tensor(line[:, a:z], line[:, a:z], peak[:, a:z], ALU.subtract).then_inc(shifted, 1)
                for i, (g, n) in enumerate(TURNS):
                    if i % 2:
                        vector.wait_ge(back, i + 1)
                        vector.tensor_copy(score[:, g:g + n, :, :].rearrange("p g h t -> p (g h t)"),
                                           p_turn[1][:, 0:n * P]).then_inc(back_out, 1)

            @block.scalar
            def _(scalar):
                for i, (g, n) in enumerate(TURNS):
                    scalar.wait_ge(turned, i + 1)
                    scalar.activation(turned_rows[:, g:g + n, :].rearrange("p g e -> p (g e)"),
                                      p_turn[i % 2][:, 0:n * P], ACT.Copy).then_inc(turned_out, 1)
                for i in range(PIECES):
                    a, z = SPAN * i // PIECES, SPAN * (i + 1) // PIECES
                    scalar.wait_ge(shifted, i + 1)
                    scalar.activation(line[:, a:z], line[:, a:z], ACT.Exp).then_inc(weights, 1)
                for i, (g, n) in enumerate(TURNS):
                    if i % 2 == 0:
                        scalar.wait_ge(back, i + 1)
                        scalar.activation(score[:, g:g + n, :, :].rearrange("p g h t -> p (g h t)"),
                                          p_turn[0][:, 0:n * P], ACT.Copy).then_inc(back_even, 1)

            @block.tensor
            def _(tensor):
                for i, (g, n) in enumerate(TURNS):
                    if i >= 2:
                        tensor.wait_ge(turned_out, i - 1)
                    for k in range(n):
                        mm = tensor.transpose(p_turn[i % 2][:, k * P:(k + 1) * P],
                                              score[:, g + k, :, :].rearrange("p h t -> p (h t)"), edges.ident[:, :])
                    mm.then_inc(turned, 1)
                for way in range(2):
                    tensor.wait_ge(ends_ready, way + 1)
                    for i in range(2):
                        mm = tensor.transpose(p_ends[0:1, i * P:(i + 1) * P], ends[:, way, i:i + 1], edges.ident[:, :])
                    mm.then_inc(ends_turned, 1)
                    tensor.wait_ge(carry_made, way + 1)
                    enters = carry_row[:, way, 0:P] if way == 0 else carry_row[:, way, 1:P + 1]
                    tensor.matmul(p_carry[:, 0:1], enters, one[:, :], start=True, stop=True).then_inc(carry_turned, 1)
                tensor.wait_ge(rows_in, 16 * HEADS)
                tensor.wait_ge(turned_out, len(TURNS))
                for i, (g, n) in enumerate(TURNS):
                    if i >= 2:
                        tensor.wait_ge(back_even if i % 2 == 0 else back_out, i // 2)
                    for k in range(n):
                        mm = tensor.transpose(p_turn[i % 2][:, k * P:(k + 1) * P], turned_rows[:, g + k, :],
                                              edges.ident[:, :])
                    mm.then_inc(back, 1)


def attend(nc, edges, weight, io, dr, out):
    RING = 4
    ROUNDS, REST = divmod(GROUPS, RING)
    with Stage(nc, "attend") as st:
        nodes = st.sb("nodes", [P, NODES], F16)
        values = st.sb("values", [P, RING * GROUP, D])
        dst_hot = st.sb("dst_hot", [P, 2, P])
        x = st.sb("x", [P, BLOCKS, D])
        w_out = st.sb("w_out", [D, D])
        b_out = st.sb("b_out", [P, D])
        inverse = st.sb("inverse", [P, HEADS])
        mean = st.sb("mean", [P, D])
        mean_t = st.sb("mean_t", [P, D])
        p_sum, p_turn, p_out = (st.ps(n, [P, BANK]) for n in ("p_sum", "p_turn", "p_out"))
        names = ("nodes_ready", "x_in", "w_in", "value_go", "pairs_ready", "pairs_free", "slots_free", "hot_ready",
                 "bias_added", "inverse_step", "mean_ready", "turned", "mean_t_ready", "out_made", "x_ready", "stored")
        (nodes_ready, x_in, w_in, value_go, pairs_ready, pairs_free, slots_free, hot_ready,
         bias_added, inverse_step, mean_ready, turned, mean_t_ready, out_made, x_ready, stored) = (st.sem(n) for n in names)
        values_in = [st.sem(f"values_in{q}") for q in range(RING)]

        with nc.Block() as block:
            @block.sync
            def _(sync):
                sync.sem_inc(pairs_free, RING * PAIRS_IN_GROUP)
                sync.dma_start(x[:, :, :], rows(dr["x3"])).then_inc(x_in, 16)
                sync.dma_start(w_out[:, :], io["wo"]).then_inc(w_in, 16)
                sync.dma_start(b_out[:, :], io["bo"].partition_broadcast(P)).then_inc(w_in, 16)

                def load(i, q):
                    sync.wait_ge(pairs_free, (i * RING + q + 1) * PAIRS_IN_GROUP)
                    sync.dma_start(values[:, q * GROUP:(q + 1) * GROUP, :],
                                   dr["values"][:, bass.ds((i * RING + q) * GROUP, GROUP), :]).then_inc(values_in[q], 16)

                with sync.Fori(0, ROUNDS) as i:
                    for q in range(RING):
                        load(i, q)
                for q in range(REST):
                    load(ROUNDS, q)
                whole = (BLOCKS - 1) * P
                sync.wait_ge(x_ready, BLOCKS)
                sync.dma_start(out[0:whole, :].rearrange("(k p) f -> p k f", p=P), x[:, 0:BLOCKS - 1, :])\
                    .then_inc(stored, 16)
                sync.dma_start(out[whole:N_NODES, :], x[0:LAST_ROWS, BLOCKS - 1, :]).then_inc(stored, 16)
                sync.wait_ge(stored, 32)

            @block.gpsimd
            def _(gpsimd):
                gpsimd.iota(nodes[:, :], pattern=[[1, NODES]], base=-CENTER, channel_multiplier=0,
                            allow_small_or_imprecise_dtypes=True).then_inc(nodes_ready, 1)
                gpsimd.wait_ge(nodes_ready, 1)

                def weigh(i, q):
                    gpsimd.wait_ge(values_in[q], 16 * i + 16)
                    gpsimd.sem_inc(value_go, 1)
                    for half in range(2):
                        t = half * PAIRS_IN_GROUP
                        v = values[:, q * GROUP + t:q * GROUP + t + 8, :].rearrange("p t (h d) -> p t h d", d=HEAD_DIM)
                        w = weight[:, bass.ds(i * RING + q, 1), :, t:t + 8].rearrange("p g h t -> p t (g h)")
                        gpsimd.tensor_tensor(v, v, w.unsqueeze(3).broadcast_to([P, 8, HEADS, HEAD_DIM]), ALU.mult)\
                              .then_inc(pairs_ready, PAIRS_IN_GROUP // 2)

                with gpsimd.Fori(0, ROUNDS) as i:
                    for q in range(RING):
                        weigh(i, q)
                for q in range(REST):
                    weigh(ROUNDS, q)

            @block.vector
            def _(vector):
                vector.wait_ge(x_in, 16)
                vector.wait_ge(w_in, 32)
                vector.tensor_tensor(x[:, :, :], x[:, :, :], b_out[:, :].unsqueeze(1).broadcast_to([P, BLOCKS, D]),
                                     ALU.add).then_inc(bias_added, 1)
                vector.wait_ge(nodes_ready, 1)

                def one_hots(b, p):
                    for k in range(2):
                        vector.wait_ge(slots_free, 2 * p + 2 * b + k + 1)
                        vector.tensor_scalar(dst_hot[:, k, :], nodes[:, bass.ds(b * P, P)],
                                             edges.dst[:, bass.ds(2 * p + k, 1)], None,
                                             ALU.is_equal).then_inc(hot_ready, 1)

                with vector.Fori(0, BLOCKS) as b:
                    first, last = block_range(vector, edges, b)
                    one_hots(b, first)
                    with vector.If(last > first):
                        with vector.Fori(first + 1, last + 1) as p:
                            one_hots(b, p)
                    vector.wait_ge(slots_free, 2 * last + 2 * b + 4)
                    vector.tensor_scalar(inverse[:, :], p_sum[:, D:D + HEADS], 1e-10, None, ALU.add)\
                          .then_inc(inverse_step, 1)
                    vector.wait_ge(inverse_step, 2 * b + 1)
                    vector.reciprocal(inverse[:, :], inverse[:, :]).then_inc(inverse_step, 1)
                    vector.wait_ge(inverse_step, 2 * b + 2)
                    vector.tensor_tensor(mean[:, :].rearrange("p (h d) -> p h d", d=HEAD_DIM),
                                         p_sum[:, 0:D].rearrange("p (h d) -> p h d", d=HEAD_DIM),
                                         inverse[:, :].unsqueeze(2).broadcast_to([P, HEADS, HEAD_DIM]),
                                         ALU.mult).then_inc(mean_ready, 1)
                    vector.wait_ge(out_made, b + 1)
                    vector.wait_ge(bias_added, 1)
                    here = x[:, bass.ds(b, 1), :].rearrange("p b f -> p (b f)")
                    vector.tensor_tensor(here, here, p_out[:, 0:D], ALU.add).then_inc(x_ready, 1)

            @block.scalar
            def _(scalar):
                with scalar.Fori(0, BLOCKS) as b:
                    scalar.wait_ge(turned, b + 1)
                    scalar.activation(mean_t[:, :], p_turn[:, 0:P], ACT.Copy).then_inc(mean_t_ready, 1)

            @block.tensor
            def _(tensor):
                tensor.sem_inc(slots_free, 2)
                tensor.wait_ge(w_in, 32)

                def sums(b, p, start):
                    tensor.wait_ge(pairs_ready, p + 1)
                    for k in range(2):
                        tensor.wait_ge(hot_ready, 2 * p + 2 * b + k + 1)
                        slot = (p % (RING * PAIRS_IN_GROUP)) * 2 + k
                        mm = tensor.matmul(p_sum[:, 0:D], dst_hot[:, k, :], values[:, bass.ds(slot, 1), :],
                                           start=start and k == 0, stop=True, skip_group_check=True)
                        if k == 0 and not start:
                            mm.then_inc(pairs_free, 1)
                        w = weight[:, bass.ds(p // PAIRS_IN_GROUP, 1), :, bass.ds((p % PAIRS_IN_GROUP) * 2 + k, 1)]
                        tensor.matmul(p_sum[:, D:D + HEADS], dst_hot[:, k, :], w.rearrange("p g h t -> p (g h t)"),
                                      start=False, stop=True, skip_group_check=True).then_inc(slots_free, 1)

                with tensor.Fori(0, BLOCKS) as b:
                    first, last = block_range(tensor, edges, b)
                    sums(b, first, True)
                    with tensor.If(last > first):
                        with tensor.Fori(first + 1, last + 1) as p:
                            sums(b, p, False)
                    tensor.wait_ge(mean_ready, b + 1)
                    tensor.transpose(p_turn[:, 0:P], mean[:, :], edges.ident[:, :]).then_inc(turned, 1)
                    tensor.wait_ge(mean_t_ready, b + 1)
                    tensor.matmul(p_out[:, 0:D], mean_t[:, :], w_out[:, :], start=True, stop=True)\
                          .then_inc(out_made, 1)
                    tensor.wait_ge(x_ready, b + 1)


def program(nc, io, out):
    Stage.used = []
    shapes = {"h0": (NODES, D), "x0": (NODES, D), "x1": (NODES, D), "x3": (NODES, D), "kv": (NODES, 2 * D),
              "q": (NODES, D), "bias": (P, TILES * HEADS), "values": (P, TILES, D), "line": (P, EDGES * HEADS // P),
              "coef": (P, BASES, TILES)}
    dr = {name: nc.dram_tensor(f"scratch_{name}", shape, F32).ap() for name, shape in shapes.items()}
    for name in ("src", "dst"):
        dr[name] = nc.dram_tensor(f"scratch_{name}", (P, TILES), F16).ap()
    dr["dst_line"] = io["dst_line"]
    with ExitStack() as whole:
        edges = Edges(nc, whole)
        with ExitStack() as dense:
            prepare(nc, edges, io, dr)
            adj = dense.enter_context(nc.sbuf_tensor("adj", [P, BLOCKS, NODES], BF16))
            relational_layer(nc, edges, adj, io, dr)
            state = dense.enter_context(nc.sbuf_tensor("state", [P, NODES], F32))
            parts = dense.enter_context(nc.sbuf_tensor("parts", [P, 3, NODES], BF16))
            enter_gated(nc, edges.ident, state, parts, io, dr)
            gated_layers(nc, adj, state, parts, io)
            Stage.clear_semaphores(nc)
            neighbour_layer(nc, edges.ident, adj, state, parts, io, dr)
        attention_tables(nc, edges.ident, io, dr)
        edges.columns(whole, "last")
        score = whole.enter_context(nc.sbuf_tensor("score", [P, GROUPS, HEADS, GROUP], F32))
        edge_scores(nc, edges, score, dr)
        softmax_weights(nc, edges, score, io, dr)
        attend(nc, edges, score, io, dr, out)


def kernel(**inputs):
    import numpy as np
    import concourse.bacc as bacc
    from concourse.bass_utils import run_bass_kernel_spmd

    a = {k: np.asarray(v) for k, v in inputs.items()}
    c = np.ascontiguousarray

    def padded(v, pad):
        o = np.full(EDGES, pad, np.int32)
        o[:N_EDGES] = v
        return o

    def columns(v, pad):
        return c(padded(v, pad).reshape(TILES, P).T)

    x = np.zeros((NODES, D), np.float32)
    x[:N_NODES] = a["x"]
    attr = np.zeros((EDGES, EDGE_F), np.float32)
    attr[:N_EDGES] = a["edge_attr_32"]
    arrays = {
        "src": columns(a["src"], 0), "dst": columns(a["dst"], NO_NODE), "etype": columns(a["edge_type_16"], 0),
        "dst_line": np.concatenate([np.int32([-1]), padded(a["dst"], NO_NODE), np.int32([-2])]),
        "x": x,
        "attr": c(attr.reshape(TILES // 4, 4, P, EDGE_F).transpose(1, 3, 0, 2)).reshape(4 * EDGE_F, TILES // 4, P),
        "self_w": a["L0_gnn_self_weight"], "bases": a["L0_gnn_bases"], "rel_w": a["L0_gnn_base_weights"].reshape(-1),
        "lin_w": c(a["L1_gnn_lin_w"].T), "lin_b": a["L1_gnn_lin_b"].reshape(D, 1), "layer_w": a["L1_gnn_weight"],
        "w_ih": c(a["L1_gnn_w_ih"].T), "w_hh": c(a["L1_gnn_w_hh"].T),
        "b_ih": c(a["L1_gnn_b_ih"].reshape(3, D).T), "b_hh": c(a["L1_gnn_b_hh"].reshape(3, D).T),
        "neigh_w": c(a["L2_gnn_W"].T), "neigh_b": a["L2_gnn_b"],
        "wq": a["L3_gnn_Wq"], "bq": a["L3_gnn_bq"], "wk": a["L3_gnn_Wk"], "bk": a["L3_gnn_bk"],
        "wv": a["L3_gnn_Wv"], "bv": a["L3_gnn_bv"], "we": a["L3_gnn_We"], "be": a["L3_gnn_be"],
        "wo": a["L3_gnn_Wo"], "bo": a["L3_gnn_bo"],
    }
    nc = bacc.Bacc("TRN2", target_bir_lowering=False, num_devices=1)
    io = {k: nc.dram_tensor(f"in_{k}", v.shape, mybir.dt.from_np(v.dtype), kind="ExternalInput").ap()
          for k, v in arrays.items()}
    out = nc.dram_tensor("out_x", (N_NODES, D), F32, kind="ExternalOutput").ap()
    program(nc, io, out)
    result = run_bass_kernel_spmd(nc, [{f"in_{k}": v for k, v in arrays.items()}], core_ids=[0])
    return result.results[0]["out_x"]
```
